# Optimizing a Trainium2 kernel written in Bass

```python
import numpy as np
import jax
import jax.numpy as jnp

def _softmax(x, axis=-1):
    return jax.nn.softmax(x, axis=axis)

def _gelu(x):
    return jax.nn.gelu(x, approximate=True)

def _silu(x):
    return jax.nn.silu(x)

def _sigmoid(x):
    return jax.nn.sigmoid(x)

def _layernorm(x, axis=-1, eps=1e-05):
    m = jnp.mean(x, axis=axis, keepdims=True)
    v = jnp.var(x, axis=axis, keepdims=True)
    return (x - m) / jnp.sqrt(v + eps)

def _scatter_add(tgt, idx, src, axis=0):
    return tgt.at[idx].add(src)

def _segment_sum(src, seg, n):
    return jax.ops.segment_sum(src, seg, n)
kernel_name = 'mk_flamingo_gated_d1_seqx_r4_38a899'

def setup_inputs(seed: int=0):
    np.random.seed(seed)
    _w = jnp.asarray

    def _rec_inputs():
        import jax
        import jax.numpy as jnp
        _rk = jax.random.key(seed)
        x = -0.0003929 + 0.9999 * jax.random.normal(jax.random.fold_in(_rk, 1), (8, 256, 256), jnp.float32)
        _lenS = 256 - jax.random.randint(jax.random.fold_in(_rk, 7), (8,), 0, max(1, 256 // 4) + 1, jnp.int32)
        _lenS2 = 256 - jax.random.randint(jax.random.fold_in(_rk, 8), (8,), 0, max(1, 256 // 4) + 1, jnp.int32)
        _ctx_512P = jax.random.normal(jax.random.fold_in(_rk, 11), (8, 16, 128), jnp.float32)
        _ctx_512c = jax.random.dirichlet(jax.random.fold_in(_rk, 511), 0.3 * jnp.ones((16,), jnp.float32), (8, 256))
        _ctx_512t = jnp.einsum('bsk,bkd->bsd', _ctx_512c, _ctx_512P)
        _ctx_512t = _ctx_512t * jax.lax.rsqrt(jnp.mean(jnp.square(_ctx_512t)) + 1e-12) * 0.953939
        ctx_512 = -1.39393e-06 + 0.999914 * (_ctx_512t + 0.3 * jax.random.normal(jax.random.fold_in(_rk, 611), (8, 256, 128), jnp.float32))
        _g = jax.random.normal(jax.random.fold_in(_rk, 9001), (2, 1), jnp.float32)
        _g = jnp.sign(_g) * jnp.maximum(jnp.abs(_g), 1.0) + (_g == 0) * 1.0
        g_xattn = _g[0]
        g_ffn = _g[1]
        return (x, ctx_512, g_xattn, g_ffn)
    x, ctx_512, g_xattn, g_ffn = _rec_inputs()

    def _L0_xattn_setup():
        import jax, jax.numpy as jnp
        import numpy as np
        HEADS = 16
        D_MODEL = 256
        IMG_MODEL = 128
        D_K = D_MODEL // HEADS
        key = jax.random.key(seed)
        ks = jax.random.split(key, 12)
        B, LQ, LKV = (8, 512, 256)
        s_dm = 1.0 / np.sqrt(D_MODEL)
        s_im = 1.0 / np.sqrt(IMG_MODEL)
        return {'q': jax.random.normal(ks[0], (B, LQ, D_MODEL), jnp.float32), 'k': jax.random.normal(ks[1], (B, LKV, IMG_MODEL), jnp.float32), 'v': jax.random.normal(ks[2], (B, LKV, IMG_MODEL), jnp.float32), 'Wq': jax.random.normal(ks[3], (D_MODEL, D_MODEL), jnp.float32) * s_dm, 'bq': jnp.zeros((D_MODEL,), jnp.float32), 'Wk': jax.random.normal(ks[4], (IMG_MODEL, D_MODEL), jnp.float32) * s_im, 'bk': jnp.zeros((D_MODEL,), jnp.float32), 'Wv': jax.random.normal(ks[5], (IMG_MODEL, D_MODEL), jnp.float32) * s_im, 'bv': jnp.zeros((D_MODEL,), jnp.float32), 'Wo': jax.random.normal(ks[6], (D_MODEL, D_MODEL), jnp.float32) * s_dm, 'bo': jnp.zeros((D_MODEL,), jnp.float32)}
    _L0_xattn_all = _L0_xattn_setup()
    _L0_xattn_in = {k: v for k, v in _L0_xattn_all.items() if k in ('Wq', 'bq', 'Wk', 'bk', 'Wv', 'bv', 'Wo', 'bo')}
    del _L0_xattn_all

    def _L0_ffn_setup():
        import jax, jax.numpy as jnp
        import numpy as np
        D_MODEL = 256
        D_FF = 704
        N_EXPERTS = 8
        key = jax.random.key(seed)
        k_in, k1, k2, k3 = jax.random.split(key, 4)
        scale = 0.02
        inputs = jax.random.normal(k_in, (4, N_EXPERTS * 512, D_MODEL), dtype=jnp.float32)
        w1 = jax.random.normal(k1, (N_EXPERTS, D_MODEL, D_FF), dtype=jnp.float32) * scale
        w3 = jax.random.normal(k3, (N_EXPERTS, D_MODEL, D_FF), dtype=jnp.float32) * scale
        w2 = jax.random.normal(k2, (N_EXPERTS, D_FF, D_MODEL), dtype=jnp.float32) * scale
        return {'inputs': inputs, 'w1': w1, 'w3': w3, 'w2': w2}
    _L0_ffn_all = _L0_ffn_setup()
    _L0_ffn_in = {k: v for k, v in _L0_ffn_all.items() if k in ('w1', 'w3', 'w2')}
    del _L0_ffn_all
    return {'x': x, 'ctx_512': ctx_512, 'g_xattn': g_xattn, 'g_ffn': g_ffn, 'L0_xattn_Wq': _L0_xattn_in['Wq'], 'L0_xattn_bq': _L0_xattn_in['bq'], 'L0_xattn_Wk': _L0_xattn_in['Wk'], 'L0_xattn_bk': _L0_xattn_in['bk'], 'L0_xattn_Wv': _L0_xattn_in['Wv'], 'L0_xattn_bv': _L0_xattn_in['bv'], 'L0_xattn_Wo': _L0_xattn_in['Wo'], 'L0_xattn_bo': _L0_xattn_in['bo'], 'L0_ffn_w1': _L0_ffn_in['w1'], 'L0_ffn_w3': _L0_ffn_in['w3'], 'L0_ffn_w2': _L0_ffn_in['w2']}

def reference(x, ctx_512, g_xattn, g_ffn, L0_xattn_Wq, L0_xattn_bq, L0_xattn_Wk, L0_xattn_bk, L0_xattn_Wv, L0_xattn_bv, L0_xattn_Wo, L0_xattn_bo, L0_ffn_w1, L0_ffn_w3, L0_ffn_w2):
    import jax
    import jax.numpy as jnp

    def _L0_xattn_ref(q, k, v, Wq, bq, Wk, bk, Wv, bv, Wo, bo):
        import jax, jax.numpy as jnp
        import numpy as np
        HEADS = 16
        D_MODEL = 256
        IMG_MODEL = 128
        D_K = D_MODEL // HEADS
        B, LQ, _ = q.shape
        LKV = k.shape[1]
        qh = (q @ Wq + bq).reshape(B, LQ, HEADS, D_K).transpose(0, 2, 1, 3)
        kh = (k @ Wk + bk).reshape(B, LKV, HEADS, D_K).transpose(0, 2, 1, 3)
        vh = (v @ Wv + bv).reshape(B, LKV, HEADS, D_K).transpose(0, 2, 1, 3)
        scale = 1.0 / np.sqrt(D_K)
        scores = jnp.einsum('bhqd,bhkd->bhqk', qh, kh) * scale
        attn = jax.nn.softmax(scores, axis=-1)
        out = jnp.einsum('bhqk,bhkd->bhqd', attn, vh)
        concat = out.transpose(0, 2, 1, 3).reshape(B, LQ, D_MODEL)
        return concat @ Wo + bo

    def _L0_ffn_ref(inputs, w1, w3, w2):
        import jax, jax.numpy as jnp
        import numpy as np
        D_MODEL = 256
        D_FF = 704
        N_EXPERTS = 8
        B, T, D = inputs.shape
        E = w1.shape[0]
        C = T // E
        x = inputs.reshape(B, E, C, D)
        gate = jnp.einsum('becd,edf->becf', x, w1)
        up = jnp.einsum('becd,edf->becf', x, w3)
        h = jax.nn.silu(gate) * up
        out = jnp.einsum('becf,efd->becd', h, w2)
        return out.reshape(B, T, D)
    x = x + jnp.tanh(g_xattn[0]) * _L0_xattn_ref(_layernorm(x, axis=-1), ctx_512, ctx_512, L0_xattn_Wq, L0_xattn_bq, L0_xattn_Wk, L0_xattn_bk, L0_xattn_Wv, L0_xattn_bv, L0_xattn_Wo, L0_xattn_bo)
    x = x + jnp.tanh(g_ffn[0]) * _L0_ffn_ref(_layernorm(x, axis=-1), L0_ffn_w1, L0_ffn_w3, L0_ffn_w2)
    return x

_drawn_inputs = setup_inputs


def setup_inputs(seed=0):
    import zlib

    import numpy as np

    out = dict(_drawn_inputs(seed))
    spreads = {'L0_xattn_bq': (0.0, 0.486),
     'L0_xattn_bk': (0.0, 0.8),
     'L0_xattn_bv': (0.0, 0.1),
     'L0_xattn_bo': (0.0, 0.1)}
    factors = {}
    for name, (base, spread) in spreads.items():
        noise = np.random.default_rng([zlib.crc32(name.encode()), seed]).standard_normal(out[name].shape)
        drawn = base * np.exp(spread * noise) if base else spread * noise
        out[name] = jnp.asarray(drawn.astype(out[name].dtype))
    for name, factor in factors.items():
        out[name] = (out[name] * factor).astype(out[name].dtype)
    return out
```

```python
from contextlib import ExitStack

import concourse.bass as bass
from concourse import mybir

F32 = mybir.dt.float32
BF16 = mybir.dt.bfloat16
ALU = mybir.AluOpType
ACT = mybir.ActivationFunctionType
AX_X = mybir.AxisListType.X

P = 128
EPS = 1e-5
PRIME = 32
PARTS = 3
Q_BLOCKS = (0, 0, 0, 1, 1, 2)
K_BLOCKS = (0, 1, 2, 0, 1, 0)


def gated_xattn_expert_ffn(nc, x, ctx_512, g_xattn, g_ffn, Wq, bq, Wk, bk, Wv, bv, Wo, bo,
                           w1, w3, w2, out):
    B, LQ, D = x.shape
    LKV, C = ctx_512.shape[1:]
    H = 16
    DK = D // H
    E, _, F = w1.shape
    TOK = LQ // E
    QT, KT, DT = LQ // P, LKV // P, D // P
    FM = F // P
    FR = F - FM * P
    FT = FM + 1
    HG = H // 4
    SLOT = P // 4
    ROWS = len(Q_BLOCKS) * DK
    MROWS = 2
    ERING = 8
    SCALE = float(DK) ** -0.5
    assert (QT, KT, DT, C, 2 * FR) == (2, 2, 2, P, P) and B % 2 == 0 and E % 2 == 0

    def shift(i, par, d):
        return i + (par + d) // 2, (par + d) % 2

    with ExitStack() as ctx:
        def sb(name, shape, dt=F32):
            return ctx.enter_context(nc.sbuf_tensor(name, shape, dt))

        def sem(name):
            return ctx.enter_context(nc.semaphore(name))

        ident = sb("ident", [P, P])
        ones = sb("ones", [P, P])
        eps = sb("eps", [P, 1])
        wq_nat = sb("wq_nat", [P, DT, D])
        wk_nat = sb("wk_nat", [P, D])
        wq_sb = sb("wq_sb", [P, DT, 2, P])
        wk_sb = sb("wk_sb", [P, 2, P])
        wv_sb = sb("wv_sb", [P, D])
        wo_sb = sb("wo_sb", [P, DT, D])
        bq_sb = sb("bq_sb", [P, 2])
        bk_sb = sb("bk_sb", [P, 2])
        bv_col = sb("bv_col", [P, DT])
        bv_wide = sb("bv_wide", [P, DT, P])
        bo_row = sb("bo_row", [P, D])
        bias_out = sb("bias_out", [P, D])
        gates = sb("gates", [P, 2])
        tanh_g = sb("tanh_g", [P, 2])

        x_in = sb("x_in", [P, QT, D])
        ctx_in = sb("ctx_in", [P, KT, C])
        bn1 = sb("bn1", [P, QT, 6])
        mv1 = sb("mv1", [P, QT, 2])
        ln1 = sb("ln1", [P, QT])
        rstd1 = sb("rstd1", [P, QT])
        xn = sb("xn", [P, QT, D])
        xT = sb("xT", [P, DT, LQ])
        cT = sb("cT", [P, LKV])
        q_parts = sb("q_parts", [P, PARTS, 2 * LQ], BF16)
        k_parts = sb("k_parts", [P, PARTS, 2 * LKV], BF16)
        q_rest = sb("q_rest", [P, 2 * LQ])
        k_rest = sb("k_rest", [P, 2 * LKV])
        q_st = sb("q_st", [P, 2, H * LQ], BF16)
        k_st = sb("k_st", [P, 2, H * LKV], BF16)
        v_sb = sb("v_sb", [P, 2, KT, H, SLOT])
        negmax = sb("negmax", [P, 2, QT, H // 2])
        mrow = sb("mrow", [H // 2, 2, MROWS, LQ], BF16)
        probs = sb("probs", [P, ERING, KT * LQ])
        u_sb = sb("u_sb", [P, HG, LQ])
        rden = sb("rden", [P, QT, H])
        attn = sb("attn", [P, QT, D])
        aT = sb("aT", [P, DT, LQ])
        x_res = sb("x_res", [P, QT, D])
        x1 = sb("x1", [P, QT, D])
        bn2 = sb("bn2", [P, QT, 6])
        mv2 = sb("mv2", [P, QT, 2])
        ln2 = sb("ln2", [P, QT])
        rstd2 = sb("rstd2", [P, QT])
        x2n = sb("x2n", [P, QT, D])
        x2T = sb("x2T", [P, DT, B * LQ])
        x1_dram = nc.dram_tensor("x1_dram", (B, LQ, D), F32, kind="Internal").ap()

        w13 = sb("w13", [P, 2, DT, 2 * F])
        w2_sb = sb("w2_sb", [P, 2, FT, D])
        x1_e = sb("x1_e", [P, 2, 2, D])
        silu = sb("silu", [P, 2, B * TOK])
        hid = sb("hid", [P, 2, FT, B * TOK])
        fin = sb("fin", [P, 2, 2, D])

        psum = ctx.enter_context(nc.psum_tensor("psum", [P, 8, 512], F32))
        sT_ps = [psum[:, i, :].rearrange("p (t q) -> p t q", t=KT) for i in (0, 1)]
        max_ps = [psum[:, i, :].rearrange("p (h k) -> p h k", h=2) for i in (2, 3)]
        u_ps = [psum[:, i, :] for i in (4, 5)]
        bank_a, bank_b = psum[:, 6, :], psum[:, 7, :]
        down_ps = [psum[:, i, :] for i in (6, 7)]

        settled = sem("settled")
        consts_ready = sem("consts_ready")
        ident_zero = sem("ident_zero")
        weights_in = sem("weights_in")
        perm_done = sem("perm_done")
        tanh_done = sem("tanh_done")
        bvw_done = sem("bvw_done")
        bvo_done = sem("bvo_done")
        bias_done = sem("bias_done")
        pads_done = sem("pads_done")
        pads_zero = sem("pads_zero")
        x_loaded = sem("x_loaded")
        ctx_loaded = sem("ctx_loaded")
        res_loaded = sem("res_loaded")
        bn1_done = sem("bn1_done")
        stats1_done = sem("stats1_done")
        ln1_done = sem("ln1_done")
        rstd1_done = sem("rstd1_done")
        xn_ready = sem("xn_ready")
        xT_done = sem("xT_done")
        xT_ready = sem("xT_ready")
        cT_done = sem("cT_done")
        cT_ready = sem("cT_ready")
        q_done = sem("q_done")
        k_done = sem("k_done")
        v_done = sem("v_done")
        q_high = sem("q_high")
        k_high = sem("k_high")
        q_rest_done = sem("q_rest_done")
        k_rest_done = sem("k_rest_done")
        mid_done = sem("mid_done")
        q_parts_done = sem("q_parts_done")
        k_parts_done = sem("k_parts_done")
        v_ready = sem("v_ready")
        q_laid = [sem(f"q_laid{i}") for i in range(2)]
        k_laid = [sem(f"k_laid{i}") for i in range(2)]
        max_scores = sem("max_scores")
        max_done = sem("max_done")
        mT_done = sem("mT_done")
        m_high = sem("m_high")
        m_parts = sem("m_parts")
        m_laid = [sem(f"m_laid{i}") for i in range(2)]
        sT_done = sem("sT_done")
        exp_done = sem("exp_done")
        pv_done = sem("pv_done")
        u_copied = sem("u_copied")
        uT_done = sem("uT_done")
        rden_done = sem("rden_done")
        attn_ready = sem("attn_ready")
        aT_done = sem("aT_done")
        aT_ready = sem("aT_ready")
        wo_done = sem("wo_done")
        res_ready = sem("res_ready")
        x1_ready = sem("x1_ready")
        x1_stored = sem("x1_stored")
        bn2_done = sem("bn2_done")
        stats2_done = sem("stats2_done")
        ln2_done = sem("ln2_done")
        rstd2_done = sem("rstd2_done")
        x2n_ready = sem("x2n_ready")
        x2T_done = sem("x2T_done")
        x2T_ready = sem("x2T_ready")
        w13_in = [sem(f"w13_in{i}") for i in range(2)]
        w2_in = [sem(f"w2_in{i}") for i in range(2)]
        x1e_in = [sem(f"x1e_in{i}") for i in range(2)]
        gu_done = sem("gu_done")
        silu_done = sem("silu_done")
        hid_done = sem("hid_done")
        down_done = sem("down_done")
        fin_done = sem("fin_done")
        out_stored = [sem(f"out_stored{i}") for i in range(2)]
        primed = (exp_done, pv_done, u_copied, uT_done, aT_done, wo_done, x1_stored, x2n_ready,
                  x2T_done, x2T_ready, xn_ready, cT_done, sT_done, xT_done, q_done, k_done, v_done,
                  q_parts_done, k_parts_done, mT_done, max_done, hid_done, down_done, fin_done,
                  *m_laid, *out_stored)

        N_CONSTS, N_WEIGHTS = 3, 10
        LAID = 16 * len(Q_BLOCKS)

        def settle(eng):
            eng.sem_inc(settled, 1)

        block = ctx.enter_context(nc.Block())

        @block.sync
        def _(sp):
            for s in primed:
                sp.sem_inc(s, PRIME)

            def load_rows(b):
                sp.wait_ge(xn_ready, PRIME + b)
                settle(sp)
                sp.dma_start(x_in[:], x[bass.ds(b, 1)].rearrange("a (t p) d -> p (a t) d", p=P))\
                    .then_inc(x_loaded, 16)
                sp.wait_ge(cT_done, PRIME + b)
                settle(sp)
                sp.dma_start(ctx_in[:], ctx_512[bass.ds(b, 1)].rearrange("a (t p) d -> p (a t) d", p=P))\
                    .then_inc(ctx_loaded, 16)

            def lay_out(i, par, st, blocks, parts, ready, laid):
                b = 2 * i + par
                sp.wait_ge(ready, PRIME + b + 1)
                settle(sp)
                sp.wait_ge(sT_done, PRIME + H * b - H)
                for n, part in enumerate(blocks):
                    sp.dma_start(st[DK * n:DK * (n + 1), par, :], parts[:, part, :])\
                        .then_inc(laid[par], 16)

            def lay_k(i, par):
                lay_out(i, par, k_st, K_BLOCKS, k_parts, k_parts_done, k_laid)

            def lay_q(i, par):
                lay_out(i, par, q_st, Q_BLOCKS, q_parts, q_parts_done, q_laid)

            def lay_max(i, par, half):
                b = 2 * i + par
                sp.wait_ge(m_parts, 2 * b + half + 1)
                for r in range(MROWS):
                    sp.dma_start(q_st[ROWS + r:ROWS + r + 1, par, half * (H // 2) * LQ:(half + 1) * (H // 2) * LQ],
                                 mrow[:, half, r, :]).then_inc(m_laid[half], 16)

            def load_weights(e, par):
                for t, (w, c0) in enumerate(((w1, 0), (w3, FM * P))):
                    src = w[bass.ds(e, 1)].rearrange("a (k p) f -> p (a k) f", p=P)
                    sp.dma_start(w13[:, par, :, c0:c0 + FM * P], src[:, :, 0:FM * P])\
                        .then_inc(w13_in[par], 16)
                    c1 = 2 * FM * P + t * FR
                    sp.dma_start(w13[:, par, :, c1:c1 + FR], src[:, :, FM * P:F]).then_inc(w13_in[par], 16)

            def load_down(e, par):
                src = w2[bass.ds(e, 1)]
                sp.dma_start(w2_sb[:, par, 0:FM, :], src[:, 0:FM * P, :].rearrange("a (m p) d -> p (a m) d", p=P))\
                    .then_inc(w2_in[par], 16)
                sp.dma_start(w2_sb[0:FR, par, FM, :], src[:, FM * P:F, :].rearrange("a p d -> p (a d)"))\
                    .then_inc(w2_in[par], 16)

            def load_x1(e, par):
                for n in range(2):
                    sp.dma_start(x1_e[:, par, n, :], x1_dram[4 * n:4 * n + 4, bass.ds(e * TOK, TOK), :])\
                        .then_inc(x1e_in[par], 16)

            def store_out(e, par):
                sp.wait_ge(fin_done, PRIME + e + 1)
                settle(sp)
                for n in range(2):
                    sp.dma_start(out[4 * n:4 * n + 4, bass.ds(e * TOK, TOK), :], fin[:, par, n, :])\
                        .then_inc(out_stored[par], 16)

            load_rows(0)
            for dst, src in ((wq_nat[:], Wq.rearrange("(k p) n -> p k n", p=P)),
                             (wk_nat[:], Wk),
                             (wv_sb[:], Wv),
                             (wo_sb[:], Wo.rearrange("(k p) n -> p k n", p=P)),
                             (bq_sb[:], bq.rearrange("(h g d) -> d h g", h=H // 2, g=2)),
                             (bk_sb[:], bk.rearrange("(h g d) -> d h g", h=H // 2, g=2)),
                             (bv_col[:], bv.rearrange("(k p) -> p k", p=P)),
                             (bo_row[:], bo.partition_broadcast(P)),
                             (gates[:, 0:1], g_xattn.partition_broadcast(P)),
                             (gates[:, 1:2], g_ffn.partition_broadcast(P))):
                sp.dma_start(dst, src, allow_slow_non_contiguous=True).then_inc(weights_in, 16)
            load_rows(1)
            lay_k(0, 0)
            lay_q(0, 0)
            lay_k(0, 1)
            lay_q(0, 1)
            lay_max(0, 0, 0)
            lay_max(0, 0, 1)
            for e in range(2):
                load_weights(e, e)
                load_down(e, e)

            def step(i, par, project, maxima):
                b = 2 * i + par
                if project:
                    load_rows(b + 2)
                sp.dma_start(x_res[:], x[bass.ds(b, 1)].rearrange("a (t p) d -> p (a t) d", p=P))\
                    .then_inc(res_loaded, 16)
                if project:
                    lay_k(i + 1, par)
                if maxima:
                    lay_max(*shift(i, par, 1), 0)
                if project:
                    lay_q(i + 1, par)
                if maxima:
                    lay_max(*shift(i, par, 1), 1)
                sp.wait_ge(x1_ready, b + 1)
                settle(sp)
                sp.dma_start(x1_dram[bass.ds(b, 1)].rearrange("a (t p) d -> p (a t) d", p=P), x1[:])\
                    .then_inc(x1_stored, 16)

            with sp.Fori(0, B // 2 - 1) as i:
                step(i, 0, True, True)
                step(i, 1, True, True)
            step(B // 2 - 1, 0, False, True)
            step(B // 2 - 1, 1, False, False)

            sp.wait_ge(x1_stored, PRIME + 16 * B)
            for e in range(2):
                load_x1(e, e)
            with sp.Fori(0, E // 2 - 1) as i:
                for par in range(2):
                    e = 2 * i + par
                    sp.wait_ge(gu_done, FT * (e + 1))
                    settle(sp)
                    load_weights(e + 2, par)
                    sp.wait_ge(down_done, PRIME + e + 1)
                    settle(sp)
                    load_down(e + 2, par)
                    store_out(e, par)
                    load_x1(e + 2, par)
            for par in range(2):
                store_out(E - 2 + par, par)
            for par in range(2):
                sp.wait_ge(out_stored[par], PRIME + 32 * (E // 2))

        @block.gpsimd
        def _(pool):
            pool.memset(ident[:], 0.0).then_inc(ident_zero, 1)
            pool.memset(ones[:], 1.0).then_inc(consts_ready, 1)
            pool.memset(eps[:], EPS).then_inc(consts_ready, 1)
            pool.wait_ge(ident_zero, 1)
            pool.affine_select(out=ident[:], in_=ident[:], compare_op=ALU.not_equal, fill=1.0, base=0,
                               pattern=[[-1, P]], channel_multiplier=1).then_inc(consts_ready, 1)
            pool.wait_ge(consts_ready, N_CONSTS)
            pool.memset(k_st[ROWS:ROWS + MROWS, :, :].bitcast(mybir.dt.uint32), 0x3F803F80).then_inc(pads_done, 1)
            pool.wait_ge(pads_done, 1)

            def norm1(b):
                pool.wait_ge(rstd1_done, b + 1)
                pool.wait_ge(xT_done, PRIME + b)
                settle(pool)
                for t in range(QT):
                    last = pool.tensor_scalar(xn[:, t, :], x_in[:, t, :], mv1[:, t, 0:1], rstd1[:, t:t + 1],
                                              ALU.subtract, ALU.mult)
                last.then_inc(xn_ready, 1)

            def cut(n, b, parts, rest, rest_done, parts_done):
                pool.wait_ge(rest_done, b + 1)
                settle(pool)
                pool.tensor_scalar(parts[:, 1, :], rest[:], 1.0, None, ALU.mult).then_inc(mid_done, 1)
                pool.wait_ge(mid_done, 2 * b + n + 1)
                pool.tensor_tensor(parts[:, 2, :], rest[:], parts[:, 1, :], ALU.subtract).then_inc(parts_done, 1)

            def cut_both(b):
                cut(0, b, q_parts, q_rest, q_rest_done, q_parts_done)
                cut(1, b, k_parts, k_rest, k_rest_done, k_parts_done)

            norm1(0)
            cut_both(0)
            norm1(1)
            pool.wait_ge(q_laid[0], LAID)
            pool.wait_ge(k_laid[0], LAID)
            cut_both(1)

            def step(i, par, project):
                b = 2 * i + par
                if project:
                    norm1(b + 2)
                pool.wait_ge(res_loaded, 16 * (b + 1))
                pool.wait_ge(bias_done, 1)
                pool.tensor_tensor(x_res[:], x_res[:], bias_out[:].unsqueeze(1).to_broadcast([P, QT, D]), ALU.add)\
                    .then_inc(res_ready, 1)
                if project:
                    ip, pp = shift(i, par, 1)
                    pool.wait_ge(q_laid[pp], LAID * (ip + 1))
                    pool.wait_ge(k_laid[pp], LAID * (ip + 1))
                    cut_both(b + 2)
                pool.wait_ge(rstd2_done, b + 1)
                pool.wait_ge(x2T_done, PRIME + b)
                settle(pool)
                for t in range(QT):
                    last = pool.tensor_scalar(x2n[:, t, :], x1[:, t, :], mv2[:, t, 0:1], rstd2[:, t:t + 1],
                                              ALU.subtract, ALU.mult)
                last.then_inc(x2n_ready, 1)

            with pool.Fori(0, B // 2 - 1) as i:
                step(i, 0, True)
                step(i, 1, True)
            step(B // 2 - 1, 0, False)
            step(B // 2 - 1, 1, False)

        @block.scalar
        def _(act):
            act.wait_ge(weights_in, 16 * N_WEIGHTS)
            act.activation(tanh_g[:], gates[:], ACT.Tanh).then_inc(tanh_done, 1)
            act.wait_ge(consts_ready, N_CONSTS)
            act.preload_act_table_set("natural_log_exp_and_others")

            def inv_std(b, mv, ln, rstd, stats_done, ln_done, rstd_done):
                act.wait_ge(stats_done, b + 1)
                act.activation(ln[:], mv[:, :, 1], ACT.Ln, bias=eps[:, 0:1]).then_inc(ln_done, 1)
                act.wait_ge(ln_done, b + 1)
                act.activation(rstd[:], ln[:], ACT.Exp, scale=-0.5).then_inc(rstd_done, 1)

            def inv_std1(b):
                inv_std(b, mv1, ln1, rstd1, stats1_done, ln1_done, rstd1_done)

            def inv_std2(b):
                inv_std(b, mv2, ln2, rstd2, stats2_done, ln2_done, rstd2_done)

            def copy_xT(b):
                act.wait_ge(xT_done, PRIME + b + 1)
                act.wait_ge(q_done, PRIME + b)
                act.activation(xT[:].rearrange("p k q -> p (k q)"), bank_a, ACT.Copy).then_inc(xT_ready, 1)

            def copy_cT(b):
                act.wait_ge(cT_done, PRIME + b + 1)
                act.wait_ge(v_done, PRIME + b)
                act.activation(cT[:], bank_b[:, 0:LKV], ACT.Copy).then_inc(cT_ready, 1)

            def high(b, bank, bias, parts, done, high_done):
                act.wait_ge(done, PRIME + b + 1)
                for g in range(2):
                    last = act.activation(parts[:, 0, g * LQ:(g + 1) * LQ], bank[:, g * LQ:(g + 1) * LQ],
                                          ACT.Identity, bias=bias[:, g:g + 1])
                last.then_inc(high_done, 1)

            def high_q(b):
                high(b, bank_b, bq_sb, q_parts, q_done, q_high)

            def high_k(b):
                high(b, bank_a, bk_sb, k_parts, k_done, k_high)

            def copy_v(b, par):
                act.wait_ge(v_done, PRIME + b + 1)
                act.activation(v_sb[:, par, :, :, 0:DK],
                               bank_a.rearrange("p (t h d) -> p t h d", t=KT, h=H), ACT.Copy).then_inc(v_ready, 1)

            for b in range(2):
                inv_std1(b)
                copy_cT(b)
                copy_xT(b)
                if b == 1:
                    act.wait_ge(q_laid[0], LAID)
                    act.wait_ge(k_laid[0], LAID)
                high_q(b)
                high_k(b)
                copy_v(b, b)

            def step(i, par, project):
                b = 2 * i + par
                ip, pp = shift(i, par, 1)

                def exp(h):
                    act.wait_ge(sT_done, PRIME + H * b + h + 1)
                    if h % 4 == 0:
                        act.wait_ge(pv_done, PRIME + HG * b + h // 4 - 1)
                    act.activation(probs[:, h % ERING, :], sT_ps[h % 2].rearrange("p t q -> p (t q)"), ACT.Exp,
                                   scale=SCALE).then_inc(exp_done, 1)

                def copy_u(n):
                    act.wait_ge(pv_done, PRIME + HG * b + 2 * n + 2)
                    act.wait_ge(uT_done, PRIME + QT * b)
                    act.activation(u_sb[:, 2 * n:2 * n + 2, :].rearrange("p g q -> p (g q)"), u_ps[n],
                                   ACT.Copy).then_inc(u_copied, 1)

                for h in range(H):
                    exp(h)
                    if project and h == 1:
                        inv_std1(b + 2)
                    if project and h == 2:
                        copy_cT(b + 2)
                    if project and h == 5:
                        copy_xT(b + 2)
                    if project and h == 8:
                        act.wait_ge(q_laid[pp], LAID * (ip + 1))
                        high_q(b + 2)
                    if project and h == 9:
                        act.wait_ge(k_laid[pp], LAID * (ip + 1))
                        high_k(b + 2)
                    if h == 10:
                        copy_u(0)
                copy_u(1)
                if project:
                    copy_v(b + 2, par)
                act.wait_ge(aT_done, PRIME + b + 1)
                act.wait_ge(wo_done, PRIME + b)
                act.activation(aT[:].rearrange("p k q -> p (k q)"), bank_b, ACT.Copy).then_inc(aT_ready, 1)
                inv_std2(b)
                act.wait_ge(x2T_done, PRIME + b + 1)
                act.activation(x2T[:, :, bass.ds(b * LQ, LQ)], bank_b.rearrange("p (k q) -> p k q", k=DT),
                               ACT.Copy).then_inc(x2T_ready, 1)

            with act.Fori(0, B // 2 - 1) as i:
                step(i, 0, True)
                step(i, 1, True)
            step(B // 2 - 1, 0, False)
            step(B // 2 - 1, 1, False)

            def gates_of(e):
                for m in range(FT):
                    act.wait_ge(gu_done, FT * e + m + 1)
                    act.wait_ge(hid_done, PRIME + FT * e + m - 1)
                    rows = P if m < FM else FR
                    act.activation(silu[0:rows, m % 2, :], psum[0:rows, m, 0:B * TOK], ACT.Silu)\
                       .then_inc(silu_done, 1)

            gates_of(0)
            with act.Fori(0, E // 2 - 1) as i:
                gates_of(2 * i + 1)
                gates_of(2 * i + 2)
            gates_of(E - 1)

        @block.vector
        def _(dve):
            def stats(b, src, bn, mv, bn_done, stats_done):
                for t in range(QT):
                    last = dve.bn_stats(bn[:, t, :], src[:, t, :])
                last.then_inc(bn_done, 1)
                dve.wait_ge(bn_done, b + 1)
                settle(dve)
                for t in range(QT):
                    last = dve.bn_aggr(mv[:, t, :], bn[:, t, :])
                last.then_inc(stats_done, 1)

            def stats1(b):
                dve.wait_ge(x_loaded, 16 * (b + 1))
                dve.wait_ge(xn_ready, PRIME + b)
                stats(b, x_in, bn1, mv1, bn1_done, stats1_done)

            def rest(b, bank, bias, parts, left, high_done, parts_done, rest_done):
                dve.wait_ge(high_done, b + 1)
                dve.wait_ge(parts_done, PRIME + b)
                for g in range(2):
                    cols = slice(g * LQ, (g + 1) * LQ)
                    last = dve.scalar_tensor_tensor(out=left[:, cols], in0=bank[:, cols], scalar=bias[:, g:g + 1],
                                                    in1=parts[:, 0, cols], op0=ALU.add, op1=ALU.subtract)
                last.then_inc(rest_done, 1)

            def rest_q(b):
                rest(b, bank_b, bq_sb, q_parts, q_rest, q_high, q_parts_done, q_rest_done)

            def rest_k(b):
                rest(b, bank_a, bk_sb, k_parts, k_rest, k_high, k_parts_done, k_rest_done)

            def row_max(b, u):
                half, pair, t = u // 8, u % 8 // 2, u % 2
                dve.wait_ge(max_scores, 16 * b + u + 1)
                if u % 8 == 0:
                    dve.wait_ge(mT_done, PRIME + 2 * b + half - 1)
                dve.tensor_reduce(negmax[:, half, t, 2 * pair:2 * pair + 2], max_ps[u % 2], AX_X, ALU.max,
                                  negate=True).then_inc(max_done, 1)

            def max_parts(b, half):
                bank = (bank_b, bank_a)[half]
                dve.wait_ge(mT_done, PRIME + 2 * b + half + 1)
                dve.wait_ge(m_laid[half], PRIME + 16 * MROWS * b)
                dve.tensor_copy(mrow[:, half, 0, :], bank[0:H // 2, 0:LQ]).then_inc(m_high, 1)
                dve.wait_ge(m_high, 2 * b + half + 1)
                dve.tensor_tensor(mrow[:, half, 1, :], bank[0:H // 2, 0:LQ], mrow[:, half, 0, :], ALU.subtract)\
                   .then_inc(m_parts, 1)

            dve.memset(v_sb[:].rearrange("p a t h c -> p (a t h c)"), 0.0).then_inc(pads_zero, 1)
            dve.memset(hid[:, :, FM, :], 0.0).then_inc(pads_zero, 1)
            dve.memset(w2_sb[FR:P, :, FM, :], 0.0).then_inc(pads_zero, 1)
            dve.wait_ge(pads_zero, 3)
            dve.memset(v_sb[:, :, :, :, DK:DK + 1].rearrange("p a t h c -> p (a t h) c"), 1.0).then_inc(pads_zero, 1)
            stats1(0)
            dve.wait_ge(weights_in, 16 * N_WEIGHTS)
            for g in range(2):
                for k in range(DT):
                    dve.tensor_copy(wq_sb[:, k, g, :].rearrange("p (d h) -> p d h", d=DK),
                                    wq_nat[:, k, :].rearrange("p (h g d) -> p g d h", g=2, d=DK)[:, g])
                last = dve.tensor_copy(wk_sb[:, g, :].rearrange("p (d h) -> p d h", d=DK),
                                       wk_nat[:].rearrange("p (h g d) -> p g d h", g=2, d=DK)[:, g])
            last.then_inc(perm_done, 1)
            dve.wait_ge(consts_ready, N_CONSTS)
            for k in range(DT):
                last = dve.tensor_scalar(bv_wide[:, k, :], ones[:], bv_col[:, k:k + 1], None, ALU.mult)
            last.then_inc(bvw_done, 1)
            rest_q(0)
            rest_k(0)
            stats1(1)
            rest_q(1)
            rest_k(1)
            for u in range(16):
                row_max(0, u)
                if u % 8 == 7:
                    max_parts(0, u // 8)
            dve.wait_ge(bvo_done, 1)
            dve.tensor_tensor(bias_out[:], u_ps[0][:, 0:D], bo_row[:], ALU.add).then_inc(bvw_done, 1)
            dve.wait_ge(bvw_done, 2)
            dve.wait_ge(tanh_done, 1)
            dve.tensor_scalar(bias_out[:], bias_out[:], tanh_g[:, 0:1], None, ALU.mult).then_inc(bias_done, 1)

            def step(i, par, project, maxima):
                b = 2 * i + par

                def divide(t):
                    bank = (bank_b, bank_a)[t].rearrange("p (h c) -> p h c", h=H)
                    dve.wait_ge(uT_done, PRIME + QT * b + t + 1)
                    dve.reciprocal(rden[:, t, :], bank[:, :, DK]).then_inc(rden_done, 1)
                    dve.wait_ge(rden_done, QT * b + t + 1)
                    if t == 0:
                        dve.wait_ge(aT_done, PRIME + b)
                    dve.tensor_tensor(attn[:, t, :].rearrange("p (h d) -> p h d", h=H), bank[:, :, 0:DK],
                                      rden[:, t, :].unsqueeze(2).to_broadcast([P, H, DK]), ALU.mult)\
                       .then_inc(attn_ready, 1)

                def residual():
                    dve.wait_ge(wo_done, PRIME + b + 1)
                    dve.wait_ge(res_ready, b + 1)
                    dve.wait_ge(x1_stored, PRIME + 16 * b)
                    dve.wait_ge(x2n_ready, PRIME + b)
                    dve.scalar_tensor_tensor(out=x1[:].rearrange("p t d -> p (t d)"), in0=bank_a,
                                             scalar=tanh_g[:, 0:1], in1=x_res[:].rearrange("p t d -> p (t d)"),
                                             op0=ALU.mult, op1=ALU.add).then_inc(x1_ready, 1)
                    dve.wait_ge(x1_ready, b + 1)
                    stats(b, x1, bn2, mv2, bn2_done, stats2_done)

                if project:
                    stats1(b + 2)
                    rest_q(b + 2)
                    rest_k(b + 2)
                for u in range(16):
                    if maxima:
                        row_max(b + 1, u)
                        if u == 7:
                            max_parts(b + 1, 0)
                    if u == 7:
                        divide(0)
                    if u == 8:
                        divide(1)
                    if u == 10:
                        residual()
                if maxima:
                    max_parts(b + 1, 1)

            with dve.Fori(0, B // 2 - 1) as i:
                step(i, 0, True, True)
                step(i, 1, True, True)
            step(B // 2 - 1, 0, False, True)
            step(B // 2 - 1, 1, False, False)

            def hidden(e, par):
                for m in range(FT):
                    dve.wait_ge(silu_done, FT * e + m + 1)
                    if m == 0:
                        dve.wait_ge(down_done, PRIME + e - 1)
                    if m < FM:
                        dve.tensor_tensor(hid[:, par, m, :], silu[:, m % 2, :], psum[:, m, B * TOK:2 * B * TOK],
                                          ALU.mult).then_inc(hid_done, 1)
                    else:
                        dve.tensor_tensor(hid[0:FR, par, m, :], silu[0:FR, m % 2, :], psum[FR:P, m, 0:B * TOK],
                                          ALU.mult).then_inc(hid_done, 1)

            def finish(e, i, par):
                dve.wait_ge(down_done, PRIME + e + 1)
                dve.wait_ge(x1e_in[par], 32 * (i + 1))
                dve.wait_ge(out_stored[par], PRIME + 32 * i)
                dve.scalar_tensor_tensor(out=fin[:, par].rearrange("p n d -> p (n d)"), in0=down_ps[par],
                                         scalar=tanh_g[:, 1:2], in1=x1_e[:, par].rearrange("p n d -> p (n d)"),
                                         op0=ALU.mult, op1=ALU.add).then_inc(fin_done, 1)

            hidden(0, 0)
            hidden(1, 1)
            finish(0, 0, 0)
            with dve.Fori(1, E // 2) as i:
                hidden(2 * i, 0)
                finish(2 * i - 1, i - 1, 1)
                hidden(2 * i + 1, 1)
                finish(2 * i, i, 0)
            finish(E - 1, E // 2 - 1, 1)

        @block.tensor
        def _(pe):
            pe.wait_ge(consts_ready, N_CONSTS)

            def transpose_ctx(b):
                pe.wait_ge(ctx_loaded, 16 * (b + 1))
                for t in range(KT):
                    last = pe.transpose(bank_b[:, t * P:(t + 1) * P], ctx_in[:, t, :], ident[:])
                last.then_inc(cT_done, 1)

            def transpose_x(b):
                pe.wait_ge(xn_ready, PRIME + b + 1)
                for k in range(DT):
                    for t in range(QT):
                        last = pe.transpose(bank_a[:, k * LQ + t * P:k * LQ + (t + 1) * P],
                                            xn[:, t, k * P:(k + 1) * P], ident[:])
                last.then_inc(xT_done, 1)

            def project_q(b):
                pe.wait_ge(xT_ready, b + 1)
                pe.wait_ge(cT_ready, b + 1)
                for g in range(2):
                    for k in range(DT):
                        last = pe.matmul(bank_b[:, g * LQ:(g + 1) * LQ], wq_sb[:, k, g, :], xT[:, k, :],
                                         start=(k == 0), stop=(k == DT - 1))
                last.then_inc(q_done, 1)

            def project_k(b):
                pe.wait_ge(cT_ready, b + 1)
                pe.wait_ge(xT_ready, b + 1)
                for g in range(2):
                    last = pe.matmul(bank_a[:, g * LKV:(g + 1) * LKV], wk_sb[:, g, :], cT[:], start=True, stop=True)
                last.then_inc(k_done, 1)

            def project_v(b):
                pe.wait_ge(k_rest_done, b + 1)
                for t in range(KT):
                    last = pe.matmul(bank_a[:, t * D:(t + 1) * D], cT[:, t * P:(t + 1) * P], wv_sb[:],
                                     start=True, stop=True)
                last.then_inc(v_done, 1)

            def score_max(i, par, u):
                b = 2 * i + par
                half, pair, t = u // 8, u % 8 // 2, u % 2
                if u == 0:
                    pe.wait_ge(q_laid[par], LAID * (i + 1))
                    pe.wait_ge(k_laid[par], LAID * (i + 1))
                pe.wait_ge(max_done, PRIME + 16 * b + u - 1)
                for n in range(2):
                    h = half * (H // 2) + 2 * pair + n
                    last = pe.matmul(max_ps[u % 2][:, n, :], q_st[0:ROWS, par, h * LQ + t * P:h * LQ + (t + 1) * P],
                                     k_st[0:ROWS, par, h * LKV:(h + 1) * LKV], start=True, stop=True)
                last.then_inc(max_scores, 1)

            def transpose_max(b, half):
                pe.wait_ge(max_done, PRIME + 16 * b + 8 * (half + 1))
                for t in range(QT):
                    last = pe.transpose((bank_b, bank_a)[half][0:H // 2, t * P:(t + 1) * P],
                                        negmax[:, half, t, :], ident[:])
                last.then_inc(mT_done, 1)

            transpose_ctx(0)
            transpose_x(0)
            pe.wait_ge(perm_done, 1)
            project_q(0)
            project_k(0)
            project_v(0)
            pe.wait_ge(q_rest_done, 1)
            transpose_ctx(1)
            pe.wait_ge(v_ready, 1)
            transpose_x(1)
            project_q(1)
            project_k(1)
            project_v(1)
            pe.wait_ge(bvw_done, 1)
            for k in range(DT):
                last = pe.matmul(u_ps[0][:, 0:D], bv_wide[:, k, :], wo_sb[:, k, :], start=(k == 0), stop=(k == DT - 1))
            last.then_inc(bvo_done, 1)
            for u in range(16):
                score_max(0, 0, u)
                if u == 7:
                    pe.wait_ge(q_rest_done, 2)
                    transpose_max(0, 0)
            pe.wait_ge(v_ready, 2)
            transpose_max(0, 1)
            pe.wait_ge(pads_done, 1)
            pe.wait_ge(pads_zero, 4)
            pe.wait_ge(bias_done, 1)

            def step(i, par, project, maxima):
                b = 2 * i + par

                def score(h):
                    if h % 8 == 0:
                        pe.wait_ge(m_laid[h // 8], PRIME + 16 * MROWS * (b + 1))
                    pe.wait_ge(exp_done, PRIME + H * b + h - 1)
                    for t in range(KT):
                        last = pe.matmul(sT_ps[h % 2][:, t, :],
                                         k_st[0:ROWS + MROWS, par, h * LKV + t * P:h * LKV + (t + 1) * P],
                                         q_st[0:ROWS + MROWS, par, h * LQ:(h + 1) * LQ], start=True, stop=True)
                    last.then_inc(sT_done, 1)

                def values(g):
                    if g == 0:
                        pe.wait_ge(v_ready, b + 1)
                    pe.wait_ge(exp_done, PRIME + H * b + 4 * g + 4)
                    if g % 2 == 0:
                        pe.wait_ge(u_copied, PRIME + 2 * b + g // 2 - 1)
                    for t in range(KT):
                        for n in range(4):
                            h = 4 * g + n
                            last = pe.matmul(u_ps[g // 2][SLOT * n:SLOT * (n + 1), g % 2 * LQ:(g % 2 + 1) * LQ],
                                             v_sb[:, par, t, h, :], probs[:, h % ERING, t * LQ:(t + 1) * LQ],
                                             start=(t == 0), stop=(t == KT - 1))
                    last.then_inc(pv_done, 1)

                def maxi(u):
                    if maxima:
                        score_max(*shift(i, par, 1), u)

                def transpose_u(t):
                    pe.wait_ge(u_copied, PRIME + 2 * b + 2)
                    for g in range(HG):
                        last = pe.transpose((bank_b, bank_a)[t][:, g * P:(g + 1) * P],
                                            u_sb[:, g, t * P:(t + 1) * P], ident[:])
                    last.then_inc(uT_done, 1)

                score(0)
                score(1)
                if project:
                    pe.wait_ge(x2T_ready, PRIME + b)
                    pe.wait_ge(m_parts, 2 * b + 1)
                    transpose_ctx(b + 2)
                for h in range(2, 6):
                    score(h)
                values(0)
                if project:
                    pe.wait_ge(m_parts, 2 * b + 2)
                    transpose_x(b + 2)
                for h in range(6, 9):
                    score(h)
                if project:
                    project_q(b + 2)
                score(9)
                values(1)
                if project:
                    project_k(b + 2)
                maxi(0)
                for h in range(10, 13):
                    score(h)
                    maxi(h - 9)
                score(13)
                values(2)
                maxi(4)
                for h in range(14, 16):
                    score(h)
                    maxi(h - 9)
                values(3)
                maxi(7)
                if maxima:
                    if project:
                        pe.wait_ge(q_rest_done, b + 3)
                    else:
                        pe.wait_ge(x2T_ready, PRIME + b)
                    transpose_max(b + 1, 0)
                if project:
                    project_v(b + 2)
                if maxima:
                    pe.wait_ge(m_parts, 2 * b + 3)
                else:
                    pe.wait_ge(x2T_ready, PRIME + b)
                transpose_u(0)
                maxi(8)
                if project:
                    pe.wait_ge(v_ready, b + 3)
                elif maxima:
                    pe.wait_ge(m_parts, 2 * b + 2)
                transpose_u(1)
                maxi(9)
                pe.wait_ge(attn_ready, QT * b + QT)
                for k in range(DT):
                    for t in range(QT):
                        last = pe.transpose(bank_b[:, k * LQ + t * P:k * LQ + (t + 1) * P],
                                            attn[:, t, k * P:(k + 1) * P], ident[:])
                last.then_inc(aT_done, 1)
                maxi(10)
                pe.wait_ge(aT_ready, b + 1)
                for t in range(QT):
                    for k in range(DT):
                        last = pe.matmul(bank_a[:, t * D:(t + 1) * D], aT[:, k, t * P:(t + 1) * P],
                                         wo_sb[:, k, :], start=(k == 0), stop=(k == DT - 1))
                last.then_inc(wo_done, 1)
                for u in range(11, 16):
                    maxi(u)
                pe.wait_ge(x2n_ready, PRIME + b + 1)
                for k in range(DT):
                    for t in range(QT):
                        last = pe.transpose(bank_b[:, k * LQ + t * P:k * LQ + (t + 1) * P],
                                            x2n[:, t, k * P:(k + 1) * P], ident[:])
                last.then_inc(x2T_done, 1)
                if maxima:
                    pe.wait_ge(x1_ready, b + 1)
                    transpose_max(b + 1, 1)

            with pe.Fori(0, B // 2 - 1) as i:
                step(i, 0, True, True)
                step(i, 1, True, True)
            step(B // 2 - 1, 0, False, True)
            step(B // 2 - 1, 1, False, False)

            pe.wait_ge(x2T_ready, PRIME + B)

            def gate_up(e, i, par):
                pe.wait_ge(w13_in[par], 64 * (i + 1))
                tok = x2T[:].rearrange("p k (b q) -> p k b q", b=B)[:, :, :, bass.ds(e * TOK, TOK)]
                for m in range(FT):
                    pe.wait_ge(hid_done, PRIME + FT * e + m + 1 - FT)
                    for n in range(2 if m < FM else 1):
                        c = n * FM * P + m * P if m < FM else 2 * FM * P
                        for k in range(DT):
                            last = pe.matmul(psum[:, m, n * B * TOK:(n + 1) * B * TOK]
                                             .rearrange("p (b q) -> p b q", b=B),
                                             w13[:, par, k, c:c + P], tok[:, k], start=(k == 0), stop=(k == DT - 1))
                    last.then_inc(gu_done, 1)

            def down(e, i, par):
                pe.wait_ge(hid_done, PRIME + FT * (e + 1))
                pe.wait_ge(w2_in[par], 32 * (i + 1))
                pe.wait_ge(fin_done, PRIME + e - 1)
                for n in range(2):
                    for m in range(FT):
                        last = pe.matmul(down_ps[par][:, n * D:(n + 1) * D], hid[:, par, m, n * P:(n + 1) * P],
                                         w2_sb[:, par, m, :], start=(m == 0), stop=(m == FT - 1))
                last.then_inc(down_done, 1)

            gate_up(0, 0, 0)
            gate_up(1, 0, 1)
            down(0, 0, 0)
            with pe.Fori(1, E // 2) as i:
                gate_up(2 * i, i, 0)
                down(2 * i - 1, i - 1, 1)
                gate_up(2 * i + 1, i, 1)
                down(2 * i, i, 0)
            down(E - 1, E // 2 - 1, 1)


_INS = ["x", "ctx_512", "g_xattn", "g_ffn", "L0_xattn_Wq", "L0_xattn_bq", "L0_xattn_Wk", "L0_xattn_bk",
        "L0_xattn_Wv", "L0_xattn_bv", "L0_xattn_Wo", "L0_xattn_bo", "L0_ffn_w1", "L0_ffn_w3", "L0_ffn_w2"]
_OUTS = [((8, 256, 256), "float32")]


def kernel(**inputs):
    import numpy as _np
    import concourse.bacc as _bacc
    from concourse import mybir as _mybir
    from concourse.bass_utils import run_bass_kernel_spmd as _run

    nc = _bacc.Bacc("TRN2", target_bir_lowering=False, num_devices=1)
    arrays, args = {}, []
    for name in _INS:
        a = _np.ascontiguousarray(inputs[name])
        arrays[f"in_{name}"] = a
        args.append(nc.dram_tensor(f"in_{name}", a.shape, _mybir.dt.from_np(a.dtype), kind="ExternalInput").ap())
    for i, (shape, dtype) in enumerate(_OUTS):
        dt = _mybir.dt.from_np(_np.dtype(dtype))
        args.append(nc.dram_tensor(f"out_{i}", shape, dt, kind="ExternalOutput").ap())
    gated_xattn_expert_ffn(nc, *args)
    r = _run(nc, [arrays], core_ids=[0])
    return r.results[0]["out_0"]
```

```python
from contextlib import ExitStack

import concourse.bass as bass
from concourse import mybir

F32 = mybir.dt.float32
BF16 = mybir.dt.bfloat16
ALU = mybir.AluOpType
ACT = mybir.ActivationFunctionType
AX_X = mybir.AxisListType.X

P = 128
EPS = 1e-5
PRIME = 32
PARTS = 3
Q_BLOCKS = (0, 0, 0, 1, 1, 2)
K_BLOCKS = (0, 1, 2, 0, 1, 0)


def gated_xattn_expert_ffn(nc, x, ctx_512, g_xattn, g_ffn, Wq, bq, Wk, bk, Wv, bv, Wo, bo,
                           w1, w3, w2, out):
    B, LQ, D = x.shape
    LKV, C = ctx_512.shape[1:]
    H = 16
    DK = D // H
    E, _, F = w1.shape
    TOK = LQ // E
    QT, KT, DT = LQ // P, LKV // P, D // P
    FM = F // P
    FR = F - FM * P
    FT = FM + 1
    HG = H // 4
    SLOT = P // 4
    ROWS = len(Q_BLOCKS) * DK
    MROWS = 2
    ERING = 8
    SCALE = float(DK) ** -0.5
    assert (QT, KT, DT, C, 2 * FR) == (2, 2, 2, P, P) and B % 2 == 0 and E % 2 == 0

    def shift(i, par, d):
        return i + (par + d) // 2, (par + d) % 2

    with ExitStack() as ctx:
        def sb(name, shape, dt=F32):
            return ctx.enter_context(nc.sbuf_tensor(name, shape, dt))

        def sem(name):
            return ctx.enter_context(nc.semaphore(name))

        ident = sb("ident", [P, P])
        ones = sb("ones", [P, P])
        eps = sb("eps", [P, 1])
        wq_nat = sb("wq_nat", [P, DT, D])
        wk_nat = sb("wk_nat", [P, D])
        wq_sb = sb("wq_sb", [P, DT, 2, P])
        wk_sb = sb("wk_sb", [P, 2, P])
        wv_sb = sb("wv_sb", [P, D])
        wo_sb = sb("wo_sb", [P, DT, D])
        bq_sb = sb("bq_sb", [P, 2])
        bk_sb = sb("bk_sb", [P, 2])
        bv_col = sb("bv_col", [P, DT])
        bv_wide = sb("bv_wide", [P, DT, P])
        bo_row = sb("bo_row", [P, D])
        bias_out = sb("bias_out", [P, D])
        gates = sb("gates", [P, 2])
        tanh_g = sb("tanh_g", [P, 2])

        x_in = sb("x_in", [P, QT, D])
        ctx_in = sb("ctx_in", [P, KT, C])
        bn1 = sb("bn1", [P, QT, 6])
        mv1 = sb("mv1", [P, QT, 2])
        ln1 = sb("ln1", [P, QT])
        rstd1 = sb("rstd1", [P, QT])
        xn = sb("xn", [P, QT, D])
        xT = sb("xT", [P, DT, LQ])
        cT = sb("cT", [P, LKV])
        q_parts = sb("q_parts", [P, PARTS, 2 * LQ], BF16)
        k_parts = sb("k_parts", [P, PARTS, 2 * LKV], BF16)
        q_rest = sb("q_rest", [P, 2 * LQ])
        k_rest = sb("k_rest", [P, 2 * LKV])
        q_st = sb("q_st", [P, 2, H * LQ], BF16)
        k_st = sb("k_st", [P, 2, H * LKV], BF16)
        v_sb = sb("v_sb", [P, 2, KT, H, SLOT])
        negmax = sb("negmax", [P, 2, QT, H // 2])
        mrow = sb("mrow", [H // 2, 2, MROWS, LQ], BF16)
        probs = sb("probs", [P, ERING, KT * LQ])
        u_sb = sb("u_sb", [P, HG, LQ])
        rden = sb("rden", [P, QT, H])
        attn = sb("attn", [P, QT, D])
        aT = sb("aT", [P, DT, LQ])
        x_res = sb("x_res", [P, QT, D])
        x1 = sb("x1", [P, QT, D])
        bn2 = sb("bn2", [P, QT, 6])
        mv2 = sb("mv2", [P, QT, 2])
        ln2 = sb("ln2", [P, QT])
        rstd2 = sb("rstd2", [P, QT])
        shift1 = sb("shift1", [P, QT])
        shift2 = sb("shift2", [P, QT])
        x2n = sb("x2n", [P, QT, D])
        x2T = sb("x2T", [P, DT, B * LQ])
        x1_dram = nc.dram_tensor("x1_dram", (B, LQ, D), F32, kind="Internal").ap()

        w13 = sb("w13", [P, 2, DT, 2 * F])
        w2_sb = sb("w2_sb", [P, 2, FT, D])
        x1_e = sb("x1_e", [P, 2, 2, D])
        silu = sb("silu", [P, 2, B * TOK])
        hid = sb("hid", [P, 2, FT, B * TOK])
        fin = sb("fin", [P, 2, 2, D])

        psum = ctx.enter_context(nc.psum_tensor("psum", [P, 8, 512], F32))
        sT_ps = [psum[:, i, :].rearrange("p (t q) -> p t q", t=KT) for i in (0, 1)]
        max_ps = [psum[:, i, :].rearrange("p (h k) -> p h k", h=2) for i in (2, 3)]
        u_ps = [psum[:, i, :] for i in (4, 5)]
        bank_a, bank_b = psum[:, 6, :], psum[:, 7, :]
        down_ps = [psum[:, i, :] for i in (6, 7)]

        settled = sem("settled")
        consts_ready = sem("consts_ready")
        ident_zero = sem("ident_zero")
        weights_in = sem("weights_in")
        perm_done = sem("perm_done")
        tanh_done = sem("tanh_done")
        bvw_done = sem("bvw_done")
        bvo_done = sem("bvo_done")
        bias_done = sem("bias_done")
        pads_done = sem("pads_done")
        pads_zero = sem("pads_zero")
        x_loaded = sem("x_loaded")
        ctx_loaded = sem("ctx_loaded")
        res_loaded = sem("res_loaded")
        bn1_done = sem("bn1_done")
        stats1_done = sem("stats1_done")
        ln1_done = sem("ln1_done")
        rstd1_done = sem("rstd1_done")
        shift1_done = sem("shift1_done")
        xn_ready = sem("xn_ready")
        xT_done = sem("xT_done")
        xT_ready = sem("xT_ready")
        cT_done = sem("cT_done")
        cT_ready = sem("cT_ready")
        q_done = sem("q_done")
        k_done = sem("k_done")
        v_done = sem("v_done")
        q_high = sem("q_high")
        k_high = sem("k_high")
        q_rest_done = sem("q_rest_done")
        k_rest_done = sem("k_rest_done")
        mid_done = sem("mid_done")
        q_parts_done = sem("q_parts_done")
        k_parts_done = sem("k_parts_done")
        v_ready = sem("v_ready")
        q_laid = [sem(f"q_laid{i}") for i in range(2)]
        k_laid = [sem(f"k_laid{i}") for i in range(2)]
        max_scores = sem("max_scores")
        max_done = sem("max_done")
        mT_done = sem("mT_done")
        m_high = sem("m_high")
        m_parts = sem("m_parts")
        m_laid = [sem(f"m_laid{i}") for i in range(2)]
        sT_done = sem("sT_done")
        exp_done = sem("exp_done")
        pv_done = sem("pv_done")
        u_copied = sem("u_copied")
        uT_done = sem("uT_done")
        rden_done = sem("rden_done")
        attn_ready = sem("attn_ready")
        aT_done = sem("aT_done")
        aT_ready = sem("aT_ready")
        wo_done = sem("wo_done")
        res_ready = sem("res_ready")
        x1_ready = sem("x1_ready")
        x1_stored = sem("x1_stored")
        bn2_done = sem("bn2_done")
        stats2_done = sem("stats2_done")
        ln2_done = sem("ln2_done")
        rstd2_done = sem("rstd2_done")
        shift2_done = sem("shift2_done")
        x2n_ready = sem("x2n_ready")
        x2T_done = sem("x2T_done")
        x2T_ready = sem("x2T_ready")
        w13_in = [sem(f"w13_in{i}") for i in range(2)]
        w2_in = [sem(f"w2_in{i}") for i in range(2)]
        x1e_in = [sem(f"x1e_in{i}") for i in range(2)]
        gu_done = sem("gu_done")
        silu_done = sem("silu_done")
        hid_done = sem("hid_done")
        down_done = sem("down_done")
        fin_done = sem("fin_done")
        out_stored = [sem(f"out_stored{i}") for i in range(2)]
        primed = (exp_done, pv_done, u_copied, uT_done, aT_done, wo_done, x1_stored, x2n_ready,
                  x2T_done, x2T_ready, xn_ready, cT_done, sT_done, xT_done, q_done, k_done, v_done,
                  q_parts_done, k_parts_done, mT_done, max_done, hid_done, down_done, fin_done,
                  *m_laid, *out_stored)

        N_CONSTS, N_WEIGHTS = 3, 10
        LAID = 16 * len(Q_BLOCKS)

        def settle(eng):
            eng.sem_inc(settled, 1)

        block = ctx.enter_context(nc.Block())

        @block.sync
        def _(sp):
            for s in primed:
                sp.sem_inc(s, PRIME)

            def load_rows(b):
                sp.wait_ge(xn_ready, PRIME + b)
                settle(sp)
                sp.dma_start(x_in[:], x[bass.ds(b, 1)].rearrange("a (t p) d -> p (a t) d", p=P))\
                    .then_inc(x_loaded, 16)
                sp.wait_ge(cT_done, PRIME + b)
                settle(sp)
                sp.dma_start(ctx_in[:], ctx_512[bass.ds(b, 1)].rearrange("a (t p) d -> p (a t) d", p=P))\
                    .then_inc(ctx_loaded, 16)

            def lay_out(i, par, st, blocks, parts, ready, laid):
                b = 2 * i + par
                sp.wait_ge(ready, PRIME + b + 1)
                settle(sp)
                sp.wait_ge(sT_done, PRIME + H * b - H)
                for n, part in enumerate(blocks):
                    sp.dma_start(st[DK * n:DK * (n + 1), par, :], parts[:, part, :])\
                        .then_inc(laid[par], 16)

            def lay_k(i, par):
                lay_out(i, par, k_st, K_BLOCKS, k_parts, k_parts_done, k_laid)

            def lay_q(i, par):
                lay_out(i, par, q_st, Q_BLOCKS, q_parts, q_parts_done, q_laid)

            def lay_max(i, par, half):
                b = 2 * i + par
                sp.wait_ge(m_parts, 2 * b + half + 1)
                for r in range(MROWS):
                    sp.dma_start(q_st[ROWS + r:ROWS + r + 1, par, half * (H // 2) * LQ:(half + 1) * (H // 2) * LQ],
                                 mrow[:, half, r, :]).then_inc(m_laid[half], 16)

            def load_weights(e, par):
                for t, (w, c0) in enumerate(((w1, 0), (w3, FM * P))):
                    src = w[bass.ds(e, 1)].rearrange("a (k p) f -> p (a k) f", p=P)
                    sp.dma_start(w13[:, par, :, c0:c0 + FM * P], src[:, :, 0:FM * P])\
                        .then_inc(w13_in[par], 16)
                    c1 = 2 * FM * P + t * FR
                    sp.dma_start(w13[:, par, :, c1:c1 + FR], src[:, :, FM * P:F]).then_inc(w13_in[par], 16)

            def load_down(e, par):
                src = w2[bass.ds(e, 1)]
                sp.dma_start(w2_sb[:, par, 0:FM, :], src[:, 0:FM * P, :].rearrange("a (m p) d -> p (a m) d", p=P))\
                    .then_inc(w2_in[par], 16)
                sp.dma_start(w2_sb[0:FR, par, FM, :], src[:, FM * P:F, :].rearrange("a p d -> p (a d)"))\
                    .then_inc(w2_in[par], 16)

            def load_x1(e, par):
                for n in range(2):
                    sp.dma_start(x1_e[:, par, n, :], x1_dram[4 * n:4 * n + 4, bass.ds(e * TOK, TOK), :])\
                        .then_inc(x1e_in[par], 16)

            def store_out(e, par):
                sp.wait_ge(fin_done, PRIME + e + 1)
                settle(sp)
                for n in range(2):
                    sp.dma_start(out[4 * n:4 * n + 4, bass.ds(e * TOK, TOK), :], fin[:, par, n, :])\
                        .then_inc(out_stored[par], 16)

            load_rows(0)
            for dst, src in ((wq_nat[:], Wq.rearrange("(k p) n -> p k n", p=P)),
                             (wk_nat[:], Wk),
                             (wv_sb[:], Wv),
                             (wo_sb[:], Wo.rearrange("(k p) n -> p k n", p=P)),
                             (bq_sb[:], bq.rearrange("(h g d) -> d h g", h=H // 2, g=2)),
                             (bk_sb[:], bk.rearrange("(h g d) -> d h g", h=H // 2, g=2)),
                             (bv_col[:], bv.rearrange("(k p) -> p k", p=P)),
                             (bo_row[:], bo.partition_broadcast(P)),
                             (gates[:, 0:1], g_xattn.partition_broadcast(P)),
                             (gates[:, 1:2], g_ffn.partition_broadcast(P))):
                sp.dma_start(dst, src, allow_slow_non_contiguous=True).then_inc(weights_in, 16)
            load_rows(1)
            lay_k(0, 0)
            lay_q(0, 0)
            lay_k(0, 1)
            load_rows(2)
            lay_max(0, 0, 0)
            lay_q(0, 1)
            for e in range(2):
                load_weights(e, e)
                load_down(e, e)

            def store_x1(b):
                sp.wait_ge(x1_ready, b + 1)
                settle(sp)
                sp.dma_start(x1_dram[bass.ds(b, 1)].rearrange("a (t p) d -> p (a t) d", p=P), x1[:])\
                    .then_inc(x1_stored, 16)

            def step(i, par, project, maxima, tail=True, load=True):
                b = 2 * i + par
                lay_max(i, par, 1)
                if maxima:
                    lay_max(*shift(i, par, 1), 0)
                if tail:
                    store_x1(b - 1)
                sp.dma_start(x_res[:], x[bass.ds(b, 1)].rearrange("a (t p) d -> p (a t) d", p=P))\
                    .then_inc(res_loaded, 16)
                if load:
                    load_rows(b + 3)
                if project:
                    lay_k(i + 1, par)
                    lay_q(i + 1, par)

            step(0, 0, True, True, tail=False)
            with sp.Fori(0, B // 2 - 2) as i:
                step(i, 1, True, True)
                step(i + 1, 0, True, True)
            step(B // 2 - 2, 1, True, True, load=False)
            step(B // 2 - 1, 0, False, True, load=False)
            step(B // 2 - 1, 1, False, False, load=False)
            store_x1(B - 1)

            sp.wait_ge(x1_stored, PRIME + 16 * B)
            for e in range(2):
                load_x1(e, e)
            with sp.Fori(0, E // 2 - 1) as i:
                for par in range(2):
                    e = 2 * i + par
                    sp.wait_ge(gu_done, FT * (e + 1))
                    settle(sp)
                    load_weights(e + 2, par)
                    sp.wait_ge(down_done, PRIME + e + 1)
                    settle(sp)
                    load_down(e + 2, par)
                    store_out(e, par)
                    load_x1(e + 2, par)
            for par in range(2):
                store_out(E - 2 + par, par)
            for par in range(2):
                sp.wait_ge(out_stored[par], PRIME + 32 * (E // 2))

        @block.gpsimd
        def _(pool):
            pool.memset(ident[:], 0.0).then_inc(ident_zero, 1)
            pool.memset(ones[:], 1.0).then_inc(consts_ready, 1)
            pool.memset(eps[:], EPS).then_inc(consts_ready, 1)
            pool.wait_ge(ident_zero, 1)
            pool.affine_select(out=ident[:], in_=ident[:], compare_op=ALU.not_equal, fill=1.0, base=0,
                               pattern=[[-1, P]], channel_multiplier=1).then_inc(consts_ready, 1)
            pool.wait_ge(consts_ready, N_CONSTS)
            pool.memset(k_st[ROWS:ROWS + MROWS, :, :].bitcast(mybir.dt.uint32), 0x3F803F80).then_inc(pads_done, 1)
            pool.wait_ge(pads_done, 1)

            def norm(src, mv, rstd, moved, moved_done, count, dst):
                pool.tensor_tensor(moved[:], mv[:, :, 0], rstd[:], ALU.mult).then_inc(moved_done, 1)
                pool.wait_ge(moved_done, 2 * count - 1)
                settle(pool)
                pool.tensor_scalar(moved[:], moved[:], -1.0, 0.0, ALU.mult, ALU.add).then_inc(moved_done, 1)
                pool.wait_ge(moved_done, 2 * count)
                settle(pool)
                for t in range(QT):
                    last = pool.tensor_scalar(dst[:, t, :], src[:, t, :], rstd[:, t:t + 1], moved[:, t:t + 1],
                                              ALU.mult, ALU.add)
                return last

            def norm1(b):
                pool.wait_ge(rstd1_done, b + 1)
                pool.wait_ge(xT_done, PRIME + b)
                settle(pool)
                norm(x_in, mv1, rstd1, shift1, shift1_done, b + 1, xn).then_inc(xn_ready, 1)

            def norm2(b):
                pool.wait_ge(rstd2_done, b + 1)
                pool.wait_ge(x2T_done, PRIME + b)
                settle(pool)
                norm(x1, mv2, rstd2, shift2, shift2_done, b + 1, x2n).then_inc(x2n_ready, 1)

            def cut(n, b, parts, rest, rest_done, parts_done):
                pool.wait_ge(rest_done, b + 1)
                settle(pool)
                pool.tensor_scalar(parts[:, 1, :], rest[:], 1.0, 0.0, ALU.mult, ALU.add).then_inc(mid_done, 1)
                pool.wait_ge(mid_done, 2 * b + n + 1)
                settle(pool)
                pool.tensor_tensor(parts[:, 2, :], rest[:], parts[:, 1, :], ALU.subtract).then_inc(parts_done, 1)

            def cut_k(b):
                cut(0, b, k_parts, k_rest, k_rest_done, k_parts_done)

            def cut_q(b):
                cut(1, b, q_parts, q_rest, q_rest_done, q_parts_done)

            for b in range(2):
                norm1(b)
                cut_k(b)
                cut_q(b)

            def step(b, project, tail=True):
                if project:
                    norm1(b + 2)
                    cut_k(b + 2)
                if tail:
                    pool.wait_ge(res_loaded, 16 * b)
                    pool.wait_ge(bias_done, 1)
                    pool.tensor_tensor(x_res[:], x_res[:], bias_out[:].unsqueeze(1).to_broadcast([P, QT, D]),
                                       ALU.add).then_inc(res_ready, 1)
                if project:
                    cut_q(b + 2)
                if tail:
                    norm2(b - 1)

            step(0, True, tail=False)
            with pool.Fori(0, B // 2 - 2) as i:
                step(2 * i + 1, True)
                step(2 * i + 2, True)
            step(B - 3, True)
            step(B - 2, False)
            step(B - 1, False)
            step(B, False)

        @block.scalar
        def _(act):
            act.wait_ge(weights_in, 16 * N_WEIGHTS)
            act.activation(tanh_g[:], gates[:], ACT.Tanh).then_inc(tanh_done, 1)
            act.wait_ge(consts_ready, N_CONSTS)
            act.preload_act_table_set("natural_log_exp_and_others")

            def inv_std(b, mv, ln, rstd, stats_done, ln_done, rstd_done):
                act.wait_ge(stats_done, b + 1)
                act.activation(ln[:], mv[:, :, 1], ACT.Ln, bias=eps[:, 0:1]).then_inc(ln_done, 1)
                act.wait_ge(ln_done, b + 1)
                act.activation(rstd[:], ln[:], ACT.Exp, scale=-0.5).then_inc(rstd_done, 1)

            def inv_std1(b):
                inv_std(b, mv1, ln1, rstd1, stats1_done, ln1_done, rstd1_done)

            def inv_std2(b):
                inv_std(b, mv2, ln2, rstd2, stats2_done, ln2_done, rstd2_done)

            def copy_xT(b):
                act.wait_ge(xT_done, PRIME + b + 1)
                act.wait_ge(q_done, PRIME + b)
                act.activation(xT[:].rearrange("p k q -> p (k q)"), bank_b, ACT.Copy).then_inc(xT_ready, 1)

            def copy_cT(b):
                act.wait_ge(cT_done, PRIME + b + 1)
                act.wait_ge(v_done, PRIME + b)
                act.activation(cT[:], bank_b[:, 0:LKV], ACT.Copy).then_inc(cT_ready, 1)

            def high(b, bank, bias, parts, done, high_done):
                act.wait_ge(done, PRIME + b + 1)
                for g in range(2):
                    last = act.activation(parts[:, 0, g * LQ:(g + 1) * LQ], bank[:, g * LQ:(g + 1) * LQ],
                                          ACT.Identity, bias=bias[:, g:g + 1])
                last.then_inc(high_done, 1)

            def high_q(b):
                high(b, bank_a, bq_sb, q_parts, q_done, q_high)

            def high_k(b):
                high(b, bank_b, bk_sb, k_parts, k_done, k_high)

            def copy_v(b, par):
                act.wait_ge(v_done, PRIME + b + 1)
                act.activation(v_sb[:, par, :, :, 0:DK],
                               bank_a.rearrange("p (t h d) -> p t h d", t=KT, h=H), ACT.Copy).then_inc(v_ready, 1)

            for b in range(2):
                copy_cT(b)
                if b == 1:
                    act.wait_ge(k_laid[0], LAID)
                high_k(b)
                inv_std1(b)
                copy_xT(b)
                if b == 1:
                    act.wait_ge(q_laid[0], LAID)
                high_q(b)
                copy_v(b, b)

            def copy_u(b, n):
                act.wait_ge(pv_done, PRIME + HG * b + 2 * n + 2)
                act.wait_ge(uT_done, PRIME + QT * b)
                act.activation(u_sb[:, 2 * n:2 * n + 2, :].rearrange("p g q -> p (g q)"), u_ps[n],
                               ACT.Copy).then_inc(u_copied, 1)

            def copy_aT(b):
                act.wait_ge(aT_done, PRIME + b + 1)
                act.wait_ge(wo_done, PRIME + b)
                act.activation(aT[:].rearrange("p k q -> p (k q)"), bank_b, ACT.Copy).then_inc(aT_ready, 1)

            def copy_x2T(b):
                act.wait_ge(x2T_done, PRIME + b + 1)
                act.activation(x2T[:, :, bass.ds(b * LQ, LQ)], bank_b.rearrange("p (k q) -> p k q", k=DT),
                               ACT.Copy).then_inc(x2T_ready, 1)

            def step(i, par, project, tail=True):
                b = 2 * i + par
                ip, pp = shift(i, par, 1)

                for h in range(H):
                    act.wait_ge(sT_done, PRIME + H * b + h + 1)
                    if h % 4 == 0:
                        act.wait_ge(pv_done, PRIME + HG * b + h // 4 - 1)
                    act.activation(probs[:, h % ERING, :], sT_ps[h % 2].rearrange("p t q -> p (t q)"), ACT.Exp,
                                   scale=SCALE).then_inc(exp_done, 1)
                    if project and h == 0:
                        inv_std1(b + 2)
                    if project and h == 1:
                        copy_cT(b + 2)
                    if project and h == 4:
                        act.wait_ge(k_laid[pp], LAID * (ip + 1))
                        high_k(b + 2)
                    if project and h == 6:
                        copy_xT(b + 2)
                    if project and h == 9:
                        act.wait_ge(q_laid[pp], LAID * (ip + 1))
                        high_q(b + 2)
                    if tail and h == 11:
                        copy_aT(b - 1)
                    if h == 12:
                        copy_u(b, 0)
                copy_u(b, 1)
                if project:
                    copy_v(b + 2, par)
                if tail:
                    inv_std2(b - 1)
                    copy_x2T(b - 1)

            step(0, 0, True, tail=False)
            with act.Fori(0, B // 2 - 2) as i:
                step(i, 1, True)
                step(i + 1, 0, True)
            step(B // 2 - 2, 1, True)
            step(B // 2 - 1, 0, False)
            step(B // 2 - 1, 1, False)
            copy_aT(B - 1)
            inv_std2(B - 1)
            copy_x2T(B - 1)

            def gates_of(e):
                for m in range(FT):
                    act.wait_ge(gu_done, FT * e + m + 1)
                    act.wait_ge(hid_done, PRIME + FT * e + m - 1)
                    rows = P if m < FM else FR
                    act.activation(silu[0:rows, m % 2, :], psum[0:rows, m, 0:B * TOK], ACT.Silu)\
                       .then_inc(silu_done, 1)

            gates_of(0)
            with act.Fori(0, E // 2 - 1) as i:
                gates_of(2 * i + 1)
                gates_of(2 * i + 2)
            gates_of(E - 1)

        @block.vector
        def _(dve):
            def stats(b, src, bn, mv, bn_done, stats_done):
                for t in range(QT):
                    last = dve.bn_stats(bn[:, t, :], src[:, t, :])
                last.then_inc(bn_done, 1)
                dve.wait_ge(bn_done, b + 1)
                settle(dve)
                for t in range(QT):
                    last = dve.bn_aggr(mv[:, t, :], bn[:, t, :])
                last.then_inc(stats_done, 1)

            def stats1(b):
                dve.wait_ge(x_loaded, 16 * (b + 1))
                dve.wait_ge(xn_ready, PRIME + b)
                stats(b, x_in, bn1, mv1, bn1_done, stats1_done)

            def rest(b, bank, bias, parts, left, high_done, parts_done, rest_done):
                dve.wait_ge(high_done, b + 1)
                dve.wait_ge(parts_done, PRIME + b)
                for g in range(2):
                    cols = slice(g * LQ, (g + 1) * LQ)
                    last = dve.scalar_tensor_tensor(out=left[:, cols], in0=bank[:, cols], scalar=bias[:, g:g + 1],
                                                    in1=parts[:, 0, cols], op0=ALU.add, op1=ALU.subtract)
                last.then_inc(rest_done, 1)

            def rest_q(b):
                rest(b, bank_a, bq_sb, q_parts, q_rest, q_high, q_parts_done, q_rest_done)

            def rest_k(b):
                rest(b, bank_b, bk_sb, k_parts, k_rest, k_high, k_parts_done, k_rest_done)

            def row_max(b, u):
                half, pair, t = u // 8, u % 8 // 2, u % 2
                dve.wait_ge(max_scores, 16 * b + u + 1)
                if u % 8 == 0:
                    dve.wait_ge(mT_done, PRIME + 2 * b + half - 1)
                dve.tensor_reduce(negmax[:, half, t, 2 * pair:2 * pair + 2], max_ps[u % 2], AX_X, ALU.max,
                                  negate=True).then_inc(max_done, 1)

            def max_parts(b, half):
                bank = (bank_b, bank_a)[half]
                dve.wait_ge(mT_done, PRIME + 2 * b + half + 1)
                dve.wait_ge(m_laid[half], PRIME + 16 * MROWS * b)
                dve.tensor_copy(mrow[:, half, 0, :], bank[0:H // 2, 0:LQ]).then_inc(m_high, 1)
                dve.wait_ge(m_high, 2 * b + half + 1)
                dve.tensor_tensor(mrow[:, half, 1, :], bank[0:H // 2, 0:LQ], mrow[:, half, 0, :], ALU.subtract)\
                   .then_inc(m_parts, 1)

            dve.memset(v_sb[:].rearrange("p a t h c -> p (a t h c)"), 0.0).then_inc(pads_zero, 1)
            dve.memset(hid[:, :, FM, :], 0.0).then_inc(pads_zero, 1)
            dve.memset(w2_sb[FR:P, :, FM, :], 0.0).then_inc(pads_zero, 1)
            dve.wait_ge(pads_zero, 3)
            dve.memset(v_sb[:, :, :, :, DK:DK + 1].rearrange("p a t h c -> p (a t h) c"), 1.0).then_inc(pads_zero, 1)
            stats1(0)
            dve.wait_ge(weights_in, 16 * N_WEIGHTS)
            for g in range(2):
                for k in range(DT):
                    dve.tensor_copy(wq_sb[:, k, g, :].rearrange("p (d h) -> p d h", d=DK),
                                    wq_nat[:, k, :].rearrange("p (h g d) -> p g d h", g=2, d=DK)[:, g])
                last = dve.tensor_copy(wk_sb[:, g, :].rearrange("p (d h) -> p d h", d=DK),
                                       wk_nat[:].rearrange("p (h g d) -> p g d h", g=2, d=DK)[:, g])
            last.then_inc(perm_done, 1)
            dve.wait_ge(consts_ready, N_CONSTS)
            for k in range(DT):
                last = dve.tensor_scalar(bv_wide[:, k, :], ones[:], bv_col[:, k:k + 1], None, ALU.mult)
            last.then_inc(bvw_done, 1)
            rest_k(0)
            stats1(1)
            rest_q(0)
            rest_k(1)
            rest_q(1)
            for u in range(16):
                row_max(0, u)
                if u == 7:
                    max_parts(0, 0)
            dve.wait_ge(bvo_done, 1)
            dve.tensor_tensor(bias_out[:], u_ps[0][:, 0:D], bo_row[:], ALU.add).then_inc(bvw_done, 1)
            dve.wait_ge(bvw_done, 2)
            dve.wait_ge(tanh_done, 1)
            dve.tensor_scalar(bias_out[:], bias_out[:], tanh_g[:, 0:1], None, ALU.mult).then_inc(bias_done, 1)

            def divide(b, t):
                bank = bank_a.rearrange("p (h c) -> p h c", h=H)
                dve.wait_ge(uT_done, PRIME + QT * b + t + 1)
                dve.reciprocal(rden[:, t, :], bank[:, :, DK]).then_inc(rden_done, 1)
                dve.wait_ge(rden_done, QT * b + t + 1)
                if t == 0:
                    dve.wait_ge(aT_done, PRIME + b)
                dve.tensor_tensor(attn[:, t, :].rearrange("p (h d) -> p h d", h=H), bank[:, :, 0:DK],
                                  rden[:, t, :].unsqueeze(2).to_broadcast([P, H, DK]), ALU.mult)\
                   .then_inc(attn_ready, 1)

            def residual(b):
                dve.wait_ge(wo_done, PRIME + b + 1)
                dve.wait_ge(res_ready, b + 1)
                dve.wait_ge(x1_stored, PRIME + 16 * b)
                dve.wait_ge(x2n_ready, PRIME + b)
                dve.scalar_tensor_tensor(out=x1[:].rearrange("p t d -> p (t d)"), in0=bank_a,
                                         scalar=tanh_g[:, 0:1], in1=x_res[:].rearrange("p t d -> p (t d)"),
                                         op0=ALU.mult, op1=ALU.add).then_inc(x1_ready, 1)
                dve.wait_ge(x1_ready, b + 1)
                stats(b, x1, bn2, mv2, bn2_done, stats2_done)

            def step(b, project, maxima, tail=True):
                max_parts(b, 1)
                if project:
                    stats1(b + 2)
                if tail:
                    divide(b - 1, 0)
                if project:
                    rest_k(b + 2)
                if tail:
                    divide(b - 1, 1)
                for u in range(16):
                    if maxima:
                        row_max(b + 1, u)
                    if project and u == 4:
                        rest_q(b + 2)
                    if maxima and u == 7:
                        max_parts(b + 1, 0)
                    if tail and u == 8:
                        residual(b - 1)

            step(0, True, True, tail=False)
            with dve.Fori(0, B // 2 - 2) as i:
                step(2 * i + 1, True, True)
                step(2 * i + 2, True, True)
            step(B - 3, True, True)
            step(B - 2, False, True)
            step(B - 1, False, False)
            divide(B - 1, 0)
            divide(B - 1, 1)
            residual(B - 1)

            def hidden(e, par):
                for m in range(FT):
                    dve.wait_ge(silu_done, FT * e + m + 1)
                    if m == 0:
                        dve.wait_ge(down_done, PRIME + e - 1)
                    if m < FM:
                        dve.tensor_tensor(hid[:, par, m, :], silu[:, m % 2, :], psum[:, m, B * TOK:2 * B * TOK],
                                          ALU.mult).then_inc(hid_done, 1)
                    else:
                        dve.tensor_tensor(hid[0:FR, par, m, :], silu[0:FR, m % 2, :], psum[FR:P, m, 0:B * TOK],
                                          ALU.mult).then_inc(hid_done, 1)

            def finish(e, i, par):
                dve.wait_ge(down_done, PRIME + e + 1)
                dve.wait_ge(x1e_in[par], 32 * (i + 1))
                dve.wait_ge(out_stored[par], PRIME + 32 * i)
                dve.scalar_tensor_tensor(out=fin[:, par].rearrange("p n d -> p (n d)"), in0=down_ps[par],
                                         scalar=tanh_g[:, 1:2], in1=x1_e[:, par].rearrange("p n d -> p (n d)"),
                                         op0=ALU.mult, op1=ALU.add).then_inc(fin_done, 1)

            hidden(0, 0)
            hidden(1, 1)
            finish(0, 0, 0)
            with dve.Fori(1, E // 2) as i:
                hidden(2 * i, 0)
                finish(2 * i - 1, i - 1, 1)
                hidden(2 * i + 1, 1)
                finish(2 * i, i, 0)
            finish(E - 1, E // 2 - 1, 1)

        @block.tensor
        def _(pe):
            pe.wait_ge(consts_ready, N_CONSTS)

            def transpose_ctx(b):
                pe.wait_ge(ctx_loaded, 16 * (b + 1))
                for t in range(KT):
                    last = pe.transpose(bank_b[:, t * P:(t + 1) * P], ctx_in[:, t, :], ident[:])
                last.then_inc(cT_done, 1)

            def project_k(b):
                pe.wait_ge(cT_ready, b + 1)
                for g in range(2):
                    last = pe.matmul(bank_b[:, g * LKV:(g + 1) * LKV], wk_sb[:, g, :], cT[:], start=True, stop=True)
                last.then_inc(k_done, 1)

            def transpose_x(b):
                pe.wait_ge(xn_ready, PRIME + b + 1)
                pe.wait_ge(k_rest_done, b + 1)
                for k in range(DT):
                    for t in range(QT):
                        last = pe.transpose(bank_b[:, k * LQ + t * P:k * LQ + (t + 1) * P],
                                            xn[:, t, k * P:(k + 1) * P], ident[:])
                last.then_inc(xT_done, 1)

            def project_q(b, g):
                pe.wait_ge(xT_ready, b + 1)
                for k in range(DT):
                    last = pe.matmul(bank_a[:, g * LQ:(g + 1) * LQ], wq_sb[:, k, g, :], xT[:, k, :],
                                     start=(k == 0), stop=(k == DT - 1))
                if g == 1:
                    last.then_inc(q_done, 1)

            def project_v(b):
                for t in range(KT):
                    last = pe.matmul(bank_a[:, t * D:(t + 1) * D], cT[:, t * P:(t + 1) * P], wv_sb[:],
                                     start=True, stop=True)
                last.then_inc(v_done, 1)

            def score_max(i, par, u):
                b = 2 * i + par
                half, pair, t = u // 8, u % 8 // 2, u % 2
                if u == 0:
                    pe.wait_ge(q_laid[par], LAID * (i + 1))
                    pe.wait_ge(k_laid[par], LAID * (i + 1))
                pe.wait_ge(max_done, PRIME + 16 * b + u - 1)
                for n in range(2):
                    h = half * (H // 2) + 2 * pair + n
                    last = pe.matmul(max_ps[u % 2][:, n, :], q_st[0:ROWS, par, h * LQ + t * P:h * LQ + (t + 1) * P],
                                     k_st[0:ROWS, par, h * LKV:(h + 1) * LKV], start=True, stop=True)
                last.then_inc(max_scores, 1)

            def transpose_max(b, half):
                pe.wait_ge(max_done, PRIME + 16 * b + 8 * (half + 1))
                for t in range(QT):
                    last = pe.transpose((bank_b, bank_a)[half][0:H // 2, t * P:(t + 1) * P],
                                        negmax[:, half, t, :], ident[:])
                last.then_inc(mT_done, 1)

            for b in range(2):
                if b == 1:
                    pe.wait_ge(xT_ready, 1)
                transpose_ctx(b)
                if b == 0:
                    pe.wait_ge(perm_done, 1)
                project_k(b)
                transpose_x(b)
                if b == 1:
                    pe.wait_ge(v_ready, 1)
                project_q(b, 0)
                project_q(b, 1)
                pe.wait_ge(q_rest_done, b + 1)
                project_v(b)
            pe.wait_ge(bvw_done, 1)
            for k in range(DT):
                last = pe.matmul(u_ps[0][:, 0:D], bv_wide[:, k, :], wo_sb[:, k, :], start=(k == 0), stop=(k == DT - 1))
            last.then_inc(bvo_done, 1)
            for u in range(16):
                score_max(0, 0, u)
                if u == 7:
                    pe.wait_ge(xT_ready, 2)
                    transpose_max(0, 0)
            pe.wait_ge(pads_done, 1)
            pe.wait_ge(pads_zero, 4)
            pe.wait_ge(bias_done, 1)

            def transpose_u(b, t):
                pe.wait_ge(u_copied, PRIME + 2 * b + 2)
                for g in range(HG):
                    last = pe.transpose(bank_a[:, g * P:(g + 1) * P], u_sb[:, g, t * P:(t + 1) * P], ident[:])
                last.then_inc(uT_done, 1)

            def transpose_attn(b):
                pe.wait_ge(attn_ready, QT * b + QT)
                for k in range(DT):
                    for t in range(QT):
                        last = pe.transpose(bank_b[:, k * LQ + t * P:k * LQ + (t + 1) * P],
                                            attn[:, t, k * P:(k + 1) * P], ident[:])
                last.then_inc(aT_done, 1)

            def project_out(b, t):
                pe.wait_ge(aT_ready, b + 1)
                for k in range(DT):
                    last = pe.matmul(bank_a[:, t * D:(t + 1) * D], aT[:, k, t * P:(t + 1) * P],
                                     wo_sb[:, k, :], start=(k == 0), stop=(k == DT - 1))
                if t == QT - 1:
                    last.then_inc(wo_done, 1)

            def transpose_x2(b):
                pe.wait_ge(x2n_ready, PRIME + b + 1)
                for k in range(DT):
                    for t in range(QT):
                        last = pe.transpose(bank_b[:, k * LQ + t * P:k * LQ + (t + 1) * P],
                                            x2n[:, t, k * P:(k + 1) * P], ident[:])
                last.then_inc(x2T_done, 1)

            def step(i, par, project, maxima, tail=True, projected=True):
                b = 2 * i + par

                def score(h):
                    if h % 8 == 0:
                        pe.wait_ge(m_laid[h // 8], PRIME + 16 * MROWS * (b + 1))
                    pe.wait_ge(exp_done, PRIME + H * b + h - 1)
                    for t in range(KT):
                        last = pe.matmul(sT_ps[h % 2][:, t, :],
                                         k_st[0:ROWS + MROWS, par, h * LKV + t * P:h * LKV + (t + 1) * P],
                                         q_st[0:ROWS + MROWS, par, h * LQ:(h + 1) * LQ], start=True, stop=True)
                    last.then_inc(sT_done, 1)

                def values(g, t):
                    if g == 0:
                        pe.wait_ge(v_ready, b + 1)
                    pe.wait_ge(exp_done, PRIME + H * b + 4 * g + 4)
                    if g % 2 == 0:
                        pe.wait_ge(u_copied, PRIME + 2 * b + g // 2 - 1)
                    for n in range(4):
                        h = 4 * g + n
                        last = pe.matmul(u_ps[g // 2][SLOT * n:SLOT * (n + 1), g % 2 * LQ:(g % 2 + 1) * LQ],
                                         v_sb[:, par, t, h, :], probs[:, h % ERING, t * LQ:(t + 1) * LQ],
                                         start=(t == 0), stop=(t == KT - 1))
                    if t == KT - 1:
                        last.then_inc(pv_done, 1)

                def maxi(u):
                    if maxima:
                        score_max(*shift(i, par, 1), u)

                if projected:
                    pe.wait_ge(v_ready, b + 2)
                else:
                    pe.wait_ge(x1_ready, b - 1)
                transpose_max(b, 1)
                score(0)
                score(1)
                if project:
                    pe.wait_ge(m_parts, 2 * b + 1)
                    pe.wait_ge(x2T_ready, PRIME + b - 1)
                    transpose_ctx(b + 2)
                score(2)
                if tail:
                    pe.wait_ge(m_parts, 2 * b + 2)
                    transpose_u(b - 1, 0)
                score(3)
                if project:
                    project_k(b + 2)
                score(4)
                score(5)
                values(0, 0)
                if tail:
                    pe.wait_ge(attn_ready, QT * b - 1)
                    transpose_u(b - 1, 1)
                score(6)
                values(0, 1)
                if project:
                    transpose_x(b + 2)
                score(7)
                maxi(0)
                score(8)
                maxi(1)
                if project:
                    if tail:
                        pe.wait_ge(attn_ready, QT * b)
                    else:
                        pe.wait_ge(m_parts, 2 * b + 2)
                    project_q(b + 2, 0)
                maxi(2)
                score(9)
                values(1, 0)
                maxi(3)
                score(10)
                values(1, 1)
                maxi(4)
                if project:
                    project_q(b + 2, 1)
                maxi(5)
                score(11)
                maxi(6)
                if tail:
                    if project:
                        pe.wait_ge(xT_ready, b + 3)
                    else:
                        pe.wait_ge(x2T_ready, PRIME + b - 1)
                    transpose_attn(b - 1)
                score(12)
                maxi(7)
                if tail:
                    if project:
                        pe.wait_ge(q_rest_done, b + 3)
                    project_out(b - 1, 0)
                score(13)
                if maxima:
                    if tail:
                        pe.wait_ge(aT_ready, b)
                    else:
                        pe.wait_ge(xT_ready, b + 3)
                    transpose_max(b + 1, 0)
                if tail:
                    project_out(b - 1, 1)
                maxi(8)
                values(2, 0)
                score(14)
                maxi(9)
                values(2, 1)
                score(15)
                maxi(10)
                if project:
                    if tail:
                        pe.wait_ge(x1_ready, b)
                    else:
                        pe.wait_ge(q_rest_done, b + 3)
                    project_v(b + 2)
                maxi(11)
                values(3, 0)
                maxi(12)
                values(3, 1)
                maxi(13)
                maxi(14)
                if tail:
                    if maxima:
                        pe.wait_ge(m_parts, 2 * b + 3)
                    else:
                        pe.wait_ge(aT_ready, b)
                    transpose_x2(b - 1)
                maxi(15)

            step(0, 0, True, True, tail=False)
            with pe.Fori(0, B // 2 - 2) as i:
                step(i, 1, True, True)
                step(i + 1, 0, True, True)
            step(B // 2 - 2, 1, True, True)
            step(B // 2 - 1, 0, False, True)
            step(B // 2 - 1, 1, False, False, projected=False)
            pe.wait_ge(x1_ready, B - 1)
            transpose_u(B - 1, 0)
            pe.wait_ge(attn_ready, QT * B - 1)
            transpose_u(B - 1, 1)
            pe.wait_ge(x2T_ready, PRIME + B - 1)
            transpose_attn(B - 1)
            for t in range(QT):
                project_out(B - 1, t)
            transpose_x2(B - 1)

            pe.wait_ge(x2T_ready, PRIME + B)

            def gate_up(e, i, par):
                pe.wait_ge(w13_in[par], 64 * (i + 1))
                tok = x2T[:].rearrange("p k (b q) -> p k b q", b=B)[:, :, :, bass.ds(e * TOK, TOK)]
                for m in range(FT):
                    pe.wait_ge(hid_done, PRIME + FT * e + m + 1 - FT)
                    for n in range(2 if m < FM else 1):
                        c = n * FM * P + m * P if m < FM else 2 * FM * P
                        for k in range(DT):
                            last = pe.matmul(psum[:, m, n * B * TOK:(n + 1) * B * TOK]
                                             .rearrange("p (b q) -> p b q", b=B),
                                             w13[:, par, k, c:c + P], tok[:, k], start=(k == 0), stop=(k == DT - 1))
                    last.then_inc(gu_done, 1)

            def down(e, i, par):
                pe.wait_ge(hid_done, PRIME + FT * (e + 1))
                pe.wait_ge(w2_in[par], 32 * (i + 1))
                pe.wait_ge(fin_done, PRIME + e - 1)
                for n in range(2):
                    for m in range(FT):
                        last = pe.matmul(down_ps[par][:, n * D:(n + 1) * D], hid[:, par, m, n * P:(n + 1) * P],
                                         w2_sb[:, par, m, :], start=(m == 0), stop=(m == FT - 1))
                last.then_inc(down_done, 1)

            gate_up(0, 0, 0)
            gate_up(1, 0, 1)
            down(0, 0, 0)
            with pe.Fori(1, E // 2) as i:
                gate_up(2 * i, i, 0)
                down(2 * i - 1, i - 1, 1)
                gate_up(2 * i + 1, i, 1)
                down(2 * i, i, 0)
            down(E - 1, E // 2 - 1, 1)


_INS = ["x", "ctx_512", "g_xattn", "g_ffn", "L0_xattn_Wq", "L0_xattn_bq", "L0_xattn_Wk", "L0_xattn_bk",
        "L0_xattn_Wv", "L0_xattn_bv", "L0_xattn_Wo", "L0_xattn_bo", "L0_ffn_w1", "L0_ffn_w3", "L0_ffn_w2"]
_OUTS = [((8, 256, 256), "float32")]


def kernel(**inputs):
    import numpy as _np
    import concourse.bacc as _bacc
    from concourse import mybir as _mybir
    from concourse.bass_utils import run_bass_kernel_spmd as _run

    nc = _bacc.Bacc("TRN2", target_bir_lowering=False, num_devices=1)
    arrays, args = {}, []
    for name in _INS:
        a = _np.ascontiguousarray(inputs[name])
        arrays[f"in_{name}"] = a
        args.append(nc.dram_tensor(f"in_{name}", a.shape, _mybir.dt.from_np(a.dtype), kind="ExternalInput").ap())
    for i, (shape, dtype) in enumerate(_OUTS):
        dt = _mybir.dt.from_np(_np.dtype(dtype))
        args.append(nc.dram_tensor(f"out_{i}", shape, dt, kind="ExternalOutput").ap())
    gated_xattn_expert_ffn(nc, *args)
    r = _run(nc, [arrays], core_ids=[0])
    return r.results[0]["out_0"]
```

```python
from contextlib import ExitStack

import concourse.bass as bass
from concourse import mybir

F32 = mybir.dt.float32
F32R = mybir.dt.float32r
BF16 = mybir.dt.bfloat16
ALU = mybir.AluOpType
ACT = mybir.ActivationFunctionType
AX_X = mybir.AxisListType.X

P = 128
EPS = 1e-5
PRIME = 32
PARTS = 3
Q_BLOCKS = (0, 0, 0, 1, 1, 2)
K_BLOCKS = (0, 1, 2, 0, 1, 0)


def gated_xattn_expert_ffn(nc, x, ctx_512, g_xattn, g_ffn, Wq, bq, Wk, bk, Wv, bv, Wo, bo,
                           w1, w3, w2, out):
    B, LQ, D = x.shape
    LKV, C = ctx_512.shape[1:]
    H = 16
    DK = D // H
    E, _, F = w1.shape
    TOK = LQ // E
    QT, KT, DT = LQ // P, LKV // P, D // P
    FM = F // P
    FR = F - FM * P
    FT = FM + 1
    HG = H // 4
    SLOT = P // 4
    ROWS = len(Q_BLOCKS) * DK
    MROWS = 2
    ERING = 8
    SCALE = float(DK) ** -0.5
    assert (QT, KT, DT, C, 2 * FR) == (2, 2, 2, P, P) and B % 2 == 0 and E % 2 == 0

    def shift(i, par, d):
        return i + (par + d) // 2, (par + d) % 2

    UNITS = 2 * H // 2
    LATE = 2
    SPLIT = ((0, 0), (0, 1), (1, 0))
    CUTS = 4
    assert CUTS == 2 * DT

    with ExitStack() as ctx:
        attention = ExitStack()

        def early(name, shape, dt=F32):
            return attention.enter_context(nc.sbuf_tensor(name, shape, dt))

        def sb(name, shape, dt=F32):
            return ctx.enter_context(nc.sbuf_tensor(name, shape, dt))

        def sem(name):
            return ctx.enter_context(nc.semaphore(name))

        ident = sb("ident", [P, P])
        ones = sb("ones", [P, P])
        eps = sb("eps", [P, 1])
        wq_nat = sb("wq_nat", [P, DT, D])
        wk_nat = sb("wk_nat", [P, D])
        wq_sb = sb("wq_sb", [P, DT, 2, P])
        wk_sb = sb("wk_sb", [P, 2, P])
        wv_sb = sb("wv_sb", [P, D])
        wo_sb = sb("wo_sb", [P, DT, D])
        bq_sb = sb("bq_sb", [P, 2])
        bk_sb = sb("bk_sb", [P, 2])
        bv_col = sb("bv_col", [P, DT])
        bv_wide = sb("bv_wide", [P, DT, P])
        bo_row = sb("bo_row", [P, D])
        bias_out = sb("bias_out", [P, D])
        gates = sb("gates", [P, 2])
        tanh_g = sb("tanh_g", [P, 2])

        x_in = sb("x_in", [P, QT, D])
        ctx_in = sb("ctx_in", [P, KT, C])
        bn1 = sb("bn1", [P, QT, 6])
        mv1 = sb("mv1", [P, QT, 2])
        ln1 = sb("ln1", [P, QT])
        rstd1 = sb("rstd1", [P, QT])
        negmax = sb("negmax", [P, 2, QT, H // 2])
        mrow = sb("mrow", [H // 2, 2, MROWS, LQ], BF16)
        rden = sb("rden", [P, QT, H])
        attn = sb("attn", [P, QT, D])
        aT = sb("aT", [P, DT, LQ])
        x_res = sb("x_res", [P, QT, D])
        x1 = sb("x1", [P, QT, D])
        bn2 = sb("bn2", [P, QT, 6])
        mv2 = sb("mv2", [P, QT, 2])
        ln2 = sb("ln2", [P, QT])
        rstd2 = sb("rstd2", [P, QT])
        shift1 = sb("shift1", [P, QT])
        shift2 = sb("shift2", [P, QT])
        x2n = sb("x2n", [P, QT, D])
        x2T = sb("x2T", [P, DT, B * LQ])
        x1_dram = nc.dram_tensor("x1_dram", (B, LQ, D), F32, kind="Internal").ap()

        w13 = sb("w13", [P, 2, DT, 2 * F])
        w2_sb = sb("w2_sb", [P, 2, FT, D])
        x1_e = sb("x1_e", [P, 2, 2, D])
        silu = sb("silu", [P, 2, B * TOK])
        hid = sb("hid", [P, 3, B * TOK])
        fin = sb("fin", [P, 2, 2, D])
        w13_cut_even = sb("w13_cut_even", [P, 2, DT, 2 * F], F32R)

        xn = early("xn", [P, QT, D])
        xT = early("xT", [P, DT, LQ])
        cT = early("cT", [P, LKV])
        q_parts = early("q_parts", [P, PARTS, 2 * LQ], BF16)
        k_parts = early("k_parts", [P, PARTS, 2 * LKV], BF16)
        q_rest = early("q_rest", [P, 2 * LQ])
        k_rest = early("k_rest", [P, 2 * LKV])
        q_st = early("q_st", [P, 2, H * LQ], BF16)
        k_st = early("k_st", [P, 2, H * LKV], BF16)
        v_sb = early("v_sb", [P, 2, KT, H, SLOT])
        probs = early("probs", [P, ERING, KT * LQ])
        u_sb = early("u_sb", [P, 2, HG, LQ])
        attention.close()

        w13_cut = [w13_cut_even, sb("w13_cut_odd", [P, 2, DT, 2 * F], F32R)]
        w2_cut = sb("w2_cut", [P, 2, 2, FT, D], F32R)
        x2_cut = sb("x2_cut", [P, 2, 2, DT, B * TOK], F32R)
        hid_cut = sb("hid_cut", [P, 2, 2, FT, B * TOK], F32R)

        psum = ctx.enter_context(nc.psum_tensor("psum", [P, 8, 512], F32))
        sT_ps = [psum[:, i, :].rearrange("p (t q) -> p t q", t=KT) for i in (0, 1)]
        max_ps = [psum[:, i, :].rearrange("p (h k) -> p h k", h=2) for i in (2, 3)]
        u_ps = [psum[:, i, :] for i in (4, 5)]
        bank_a, bank_b = psum[:, 6, :], psum[:, 7, :]
        down_ps = [psum[:, i, :] for i in (6, 7)]

        settled = sem("settled")
        consts_ready = sem("consts_ready")
        ident_zero = sem("ident_zero")
        gates_in = sem("gates_in")
        qk_in = sem("qk_in")
        weights_in = sem("weights_in")
        perm_done = sem("perm_done")
        tanh_done = sem("tanh_done")
        bvw_done = sem("bvw_done")
        bvo_done = sem("bvo_done")
        bias_done = sem("bias_done")
        pads_done = sem("pads_done")
        pads_zero = sem("pads_zero")
        x_loaded = sem("x_loaded")
        ctx_loaded = sem("ctx_loaded")
        res_loaded = sem("res_loaded")
        bn1_done = sem("bn1_done")
        stats1_done = sem("stats1_done")
        ln1_done = sem("ln1_done")
        rstd1_done = sem("rstd1_done")
        shift1_done = sem("shift1_done")
        xn_ready = sem("xn_ready")
        xT_done = sem("xT_done")
        xT_ready = sem("xT_ready")
        cT_done = sem("cT_done")
        cT_ready = sem("cT_ready")
        q_done = sem("q_done")
        k_done = sem("k_done")
        v_done = sem("v_done")
        q_high = sem("q_high")
        k_high = sem("k_high")
        q_rest_done = sem("q_rest_done")
        k_rest_done = sem("k_rest_done")
        mid_done = sem("mid_done")
        q_parts_done = sem("q_parts_done")
        k_parts_done = sem("k_parts_done")
        v_ready = sem("v_ready")
        q_laid = [sem(f"q_laid{i}") for i in range(2)]
        k_laid = [sem(f"k_laid{i}") for i in range(2)]
        max_scores = sem("max_scores")
        max_done = sem("max_done")
        mT_done = sem("mT_done")
        m_high = sem("m_high")
        m_parts = sem("m_parts")
        m_laid = [sem(f"m_laid{i}") for i in range(2)]
        sT_done = sem("sT_done")
        exp_done = sem("exp_done")
        pv_done = sem("pv_done")
        u_copied = sem("u_copied")
        uT_done = sem("uT_done")
        rden_done = sem("rden_done")
        attn_ready = sem("attn_ready")
        aT_done = sem("aT_done")
        aT_ready = sem("aT_ready")
        wo_done = sem("wo_done")
        res_ready = sem("res_ready")
        x1_ready = sem("x1_ready")
        x1_stored = sem("x1_stored")
        bn2_done = sem("bn2_done")
        stats2_done = sem("stats2_done")
        ln2_done = sem("ln2_done")
        rstd2_done = sem("rstd2_done")
        shift2_done = sem("shift2_done")
        x2n_ready = sem("x2n_ready")
        x2T_done = sem("x2T_done")
        x2T_ready = sem("x2T_ready")
        w13_in = [sem(f"w13_in{i}") for i in range(2)]
        w2_in = [sem(f"w2_in{i}") for i in range(2)]
        x1e_in = [sem(f"x1e_in{i}") for i in range(2)]
        gu_done = sem("gu_done")
        silu_done = sem("silu_done")
        hid_done = sem("hid_done")
        w13_high = sem("w13_high")
        w13_low = sem("w13_low")
        w2_high = sem("w2_high")
        w2_low = sem("w2_low")
        x2_high = sem("x2_high")
        x2_low = sem("x2_low")
        hid_high = sem("hid_high")
        hid_low = sem("hid_low")
        down_done = sem("down_done")
        fin_done = sem("fin_done")
        out_stored = [sem(f"out_stored{i}") for i in range(2)]
        primed = (exp_done, pv_done, u_copied, uT_done, aT_done, wo_done, x1_stored, x2n_ready,
                  x2T_done, x2T_ready, xn_ready, cT_done, sT_done, xT_done, q_done, k_done, v_done,
                  q_parts_done, k_parts_done, mT_done, max_done, hid_done, hid_low, down_done, fin_done,
                  *m_laid, *out_stored)

        N_CONSTS, N_GATES, N_QK, N_WEIGHTS = 3, 2, 4, 4
        LAID = 16 * len(Q_BLOCKS)

        def tokens(e):
            return x2T[:].rearrange("p k (b q) -> p k b q", b=B)[:, :, :, bass.ds(e * TOK, TOK)]

        def hid_slot(m):
            return m % 2 if m < FM else 2

        def piece(c):
            return c // 2, slice(c % 2 * F, (c % 2 + 1) * F)

        def settle(eng):
            eng.sem_inc(settled, 1)

        block = ctx.enter_context(nc.Block())

        @block.sync
        def _(sp):
            for s in primed:
                sp.sem_inc(s, PRIME)

            def load_rows(b):
                sp.wait_ge(xn_ready, PRIME + b)
                settle(sp)
                sp.dma_start(x_in[:], x[bass.ds(b, 1)].rearrange("a (t p) d -> p (a t) d", p=P))\
                    .then_inc(x_loaded, 16)
                sp.wait_ge(cT_done, PRIME + b)
                settle(sp)
                sp.dma_start(ctx_in[:], ctx_512[bass.ds(b, 1)].rearrange("a (t p) d -> p (a t) d", p=P))\
                    .then_inc(ctx_loaded, 16)

            def lay_out(i, par, st, blocks, parts, ready, laid):
                b = 2 * i + par
                sp.wait_ge(ready, PRIME + b + 1)
                settle(sp)
                sp.wait_ge(sT_done, PRIME + H * b - H)
                for n, part in enumerate(blocks):
                    sp.dma_start(st[DK * n:DK * (n + 1), par, :], parts[:, part, :])\
                        .then_inc(laid[par], 16)

            def lay_k(i, par):
                lay_out(i, par, k_st, K_BLOCKS, k_parts, k_parts_done, k_laid)

            def lay_q(i, par):
                lay_out(i, par, q_st, Q_BLOCKS, q_parts, q_parts_done, q_laid)

            def lay_max(i, par, half):
                b = 2 * i + par
                sp.wait_ge(m_parts, 2 * b + half + 1)
                for r in range(MROWS):
                    sp.dma_start(q_st[ROWS + r:ROWS + r + 1, par, half * (H // 2) * LQ:(half + 1) * (H // 2) * LQ],
                                 mrow[:, half, r, :]).then_inc(m_laid[half], 16)

            def load_weights(e, par):
                for t, (w, c0) in enumerate(((w1, 0), (w3, FM * P))):
                    src = w[bass.ds(e, 1)].rearrange("a (k p) f -> p (a k) f", p=P)
                    sp.dma_start(w13[:, par, :, c0:c0 + FM * P], src[:, :, 0:FM * P])\
                        .then_inc(w13_in[par], 16)
                    c1 = 2 * FM * P + t * FR
                    sp.dma_start(w13[:, par, :, c1:c1 + FR], src[:, :, FM * P:F]).then_inc(w13_in[par], 16)

            def load_down(e, par):
                src = w2[bass.ds(e, 1)]
                sp.dma_start(w2_sb[:, par, 0:FM, :], src[:, 0:FM * P, :].rearrange("a (m p) d -> p (a m) d", p=P))\
                    .then_inc(w2_in[par], 16)
                sp.dma_start(w2_sb[0:FR, par, FM, :], src[:, FM * P:F, :].rearrange("a p d -> p (a d)"))\
                    .then_inc(w2_in[par], 16)

            def load_x1(e, par):
                for n in range(2):
                    sp.dma_start(x1_e[:, par, n, :], x1_dram[4 * n:4 * n + 4, bass.ds(e * TOK, TOK), :])\
                        .then_inc(x1e_in[par], 16)

            def store_out(e, par):
                sp.wait_ge(fin_done, PRIME + e + 1)
                settle(sp)
                for n in range(2):
                    sp.dma_start(out[4 * n:4 * n + 4, bass.ds(e * TOK, TOK), :], fin[:, par, n, :])\
                        .then_inc(out_stored[par], 16)

            def load_weight(dst, src, loaded):
                sp.dma_start(dst, src, allow_slow_non_contiguous=True).then_inc(loaded, 16)

            load_rows(0)
            load_weight(gates[:, 0:1], g_xattn.partition_broadcast(P), gates_in)
            load_weight(gates[:, 1:2], g_ffn.partition_broadcast(P), gates_in)
            load_weight(wk_nat[:], Wk, qk_in)
            load_weight(bk_sb[:], bk.rearrange("(h g d) -> d h g", h=H // 2, g=2), qk_in)
            load_weight(wq_nat[:], Wq.rearrange("(k p) n -> p k n", p=P), qk_in)
            load_weight(bq_sb[:], bq.rearrange("(h g d) -> d h g", h=H // 2, g=2), qk_in)
            load_weight(wv_sb[:], Wv, weights_in)
            load_rows(1)
            load_weight(wo_sb[:], Wo.rearrange("(k p) n -> p k n", p=P), weights_in)
            load_weight(bv_col[:], bv.rearrange("(k p) -> p k", p=P), weights_in)
            load_weight(bo_row[:], bo.partition_broadcast(P), weights_in)
            lay_k(0, 0)
            lay_q(0, 0)
            load_rows(2)
            lay_k(0, 1)
            lay_q(0, 1)
            lay_max(0, 0, 0)

            def store_x1(b):
                sp.wait_ge(x1_ready, b + 1)
                settle(sp)
                sp.dma_start(x1_dram[bass.ds(b, 1)].rearrange("a (t p) d -> p (a t) d", p=P), x1[:])\
                    .then_inc(x1_stored, 16)

            def step(i, par, normed, project, maxima, first=False):
                b = 2 * i + par
                if normed:
                    load_rows(b + 3)
                lay_max(i, par, 1)
                if project:
                    lay_k(i + 1, par)
                if maxima:
                    lay_max(*shift(i, par, 1), 0)
                if project:
                    lay_q(i + 1, par)
                if not first:
                    store_x1(b - 1)
                sp.dma_start(x_res[:], x[bass.ds(b, 1)].rearrange("a (t p) d -> p (a t) d", p=P))\
                    .then_inc(res_loaded, 16)

            step(0, 0, True, True, True, first=True)
            with sp.Fori(0, B // 2 - 2) as i:
                step(i, 1, True, True, True)
                step(i + 1, 0, True, True, True)
            step(B // 2 - 2, 1, False, True, True)
            step(B // 2 - 1, 0, False, False, True)
            step(B // 2 - 1, 1, False, False, False)
            for e in range(2):
                load_weights(e, e)
                load_down(e, e)
            store_x1(B - 1)

            sp.wait_ge(x1_stored, PRIME + 16 * B)
            for e in range(2):
                load_x1(e, e)
            def reload(e, par, weights=True):
                if weights:
                    sp.wait_ge(w13_low, CUTS * (e + 2))
                    settle(sp)
                    load_weights(e + 3, 1 - par)
                sp.wait_ge(w2_low, e + 1)
                settle(sp)
                load_down(e + 2, par)
                store_out(e, par)
                load_x1(e + 2, par)

            sp.wait_ge(w13_low, CUTS)
            load_weights(2, 0)
            with sp.Fori(0, E // 2 - 2) as i:
                reload(2 * i, 0)
                reload(2 * i + 1, 1)
            reload(E - 4, 0)
            reload(E - 3, 1, weights=False)
            for par in range(2):
                store_out(E - 2 + par, par)
            for par in range(2):
                sp.wait_ge(out_stored[par], PRIME + 32 * (E // 2))

        @block.gpsimd
        def _(pool):
            pool.memset(ident[:], 0.0).then_inc(ident_zero, 1)
            pool.memset(ones[:], 1.0).then_inc(consts_ready, 1)
            pool.memset(eps[:], EPS).then_inc(consts_ready, 1)
            pool.wait_ge(ident_zero, 1)
            pool.affine_select(out=ident[:], in_=ident[:], compare_op=ALU.not_equal, fill=1.0, base=0,
                               pattern=[[-1, P]], channel_multiplier=1).then_inc(consts_ready, 1)
            pool.wait_ge(consts_ready, N_CONSTS)
            pool.memset(k_st[ROWS:ROWS + MROWS, :, :].bitcast(mybir.dt.uint32), 0x3F803F80).then_inc(pads_done, 1)
            pool.wait_ge(pads_done, 1)

            def norm(src, mv, rstd, moved, moved_done, count, dst):
                pool.tensor_tensor(moved[:], mv[:, :, 0], rstd[:], ALU.mult).then_inc(moved_done, 1)
                pool.wait_ge(moved_done, 2 * count - 1)
                settle(pool)
                pool.tensor_scalar(moved[:], moved[:], -1.0, 0.0, ALU.mult, ALU.add).then_inc(moved_done, 1)
                pool.wait_ge(moved_done, 2 * count)
                settle(pool)
                for t in range(QT):
                    last = pool.tensor_scalar(dst[:, t, :], src[:, t, :], rstd[:, t:t + 1], moved[:, t:t + 1],
                                              ALU.mult, ALU.add)
                return last

            def norm1(b):
                pool.wait_ge(rstd1_done, b + 1)
                pool.wait_ge(xT_done, PRIME + b)
                settle(pool)
                norm(x_in, mv1, rstd1, shift1, shift1_done, b + 1, xn).then_inc(xn_ready, 1)

            def norm2(b):
                pool.wait_ge(rstd2_done, b + 1)
                pool.wait_ge(x2T_done, PRIME + b)
                settle(pool)
                norm(x1, mv2, rstd2, shift2, shift2_done, b + 1, x2n).then_inc(x2n_ready, 1)

            def cut(n, b, parts, rest, rest_done, parts_done):
                pool.wait_ge(rest_done, b + 1)
                settle(pool)
                pool.tensor_scalar(parts[:, 1, :], rest[:], 1.0, 0.0, ALU.mult, ALU.add).then_inc(mid_done, 1)
                pool.wait_ge(mid_done, 2 * b + n + 1)
                settle(pool)
                pool.tensor_tensor(parts[:, 2, :], rest[:], parts[:, 1, :], ALU.subtract).then_inc(parts_done, 1)

            def cut_k(b):
                cut(0, b, k_parts, k_rest, k_rest_done, k_parts_done)

            def cut_q(b):
                cut(1, b, q_parts, q_rest, q_rest_done, q_parts_done)

            norm1(0)
            cut_k(0)
            norm1(1)
            cut_q(0)
            cut_k(1)
            cut_q(1)
            norm1(2)

            def add_bias(b):
                pool.wait_ge(res_loaded, 16 * (b + 1))
                pool.wait_ge(bias_done, 1)
                pool.tensor_tensor(x_res[:], x_res[:], bias_out[:].unsqueeze(1).to_broadcast([P, QT, D]),
                                   ALU.add).then_inc(res_ready, 1)

            def step(b, normed, project, first=False):
                if project:
                    cut_k(b + 2)
                if not first:
                    add_bias(b - 1)
                if project:
                    cut_q(b + 2)
                if normed:
                    norm1(b + 3)
                if not first:
                    norm2(b - 1)

            step(0, True, True, first=True)
            with pool.Fori(0, B // 2 - 2) as i:
                step(2 * i + 1, True, True)
                step(2 * i + 2, True, True)
            step(B - 3, False, True)
            step(B - 2, False, False)
            step(B - 1, False, False)
            add_bias(B - 1)
            norm2(B - 1)

            def cut_x2(e, par, count, b0=0, b1=B):
                pool.wait_ge(x2_high, count)
                high, low = (x2_cut[:, par, n].rearrange("p k (b q) -> p k b q", b=B)[:, :, b0:b1] for n in (0, 1))
                pool.tensor_tensor(low, tokens(e)[:, :, b0:b1], high.bitcast(F32), ALU.subtract).then_inc(x2_low, 1)

            def expert(e, par, more=True):
                for m in range(FT):
                    pool.wait_ge(hid_high, FT * e + m + 1)
                    pool.tensor_tensor(hid_cut[:, par, 1, m, :], hid[:, hid_slot(m), :],
                                       hid_cut[:, par, 0, m, :].bitcast(F32), ALU.subtract).then_inc(hid_low, 1)
                    if more and m == 3:
                        cut_x2(e + 1, 1 - par, e + 3)

            cut_x2(0, 0, 1, 0, B - 1)
            cut_x2(0, 0, 2, B - 1, B)
            expert(0, 0)
            with pool.Fori(0, E // 2 - 1) as i:
                expert(2 * i + 1, 1)
                expert(2 * i + 2, 0)
            expert(E - 1, 1, more=False)

        @block.scalar
        def _(act):
            act.wait_ge(gates_in, 16 * N_GATES)
            act.activation(tanh_g[:], gates[:], ACT.Tanh).then_inc(tanh_done, 1)
            act.wait_ge(consts_ready, N_CONSTS)
            act.preload_act_table_set("natural_log_exp_and_others")

            def inv_std(b, mv, ln, rstd, stats_done, ln_done, rstd_done):
                act.wait_ge(stats_done, b + 1)
                act.activation(ln[:], mv[:, :, 1], ACT.Ln, bias=eps[:, 0:1]).then_inc(ln_done, 1)
                act.wait_ge(ln_done, b + 1)
                act.activation(rstd[:], ln[:], ACT.Exp, scale=-0.5).then_inc(rstd_done, 1)

            def inv_std1(b):
                inv_std(b, mv1, ln1, rstd1, stats1_done, ln1_done, rstd1_done)

            def inv_std2(b):
                inv_std(b, mv2, ln2, rstd2, stats2_done, ln2_done, rstd2_done)

            def copy_xT(b):
                act.wait_ge(xT_done, PRIME + b + 1)
                act.wait_ge(q_done, PRIME + b)
                act.activation(xT[:].rearrange("p k q -> p (k q)"), bank_a, ACT.Copy).then_inc(xT_ready, 1)

            def copy_cT(b):
                act.wait_ge(cT_done, PRIME + b + 1)
                act.wait_ge(v_done, PRIME + b)
                act.activation(cT[:], bank_b[:, 0:LKV], ACT.Copy).then_inc(cT_ready, 1)

            def high(b, bank, bias, parts, done, high_done):
                act.wait_ge(done, PRIME + b + 1)
                for g in range(2):
                    last = act.activation(parts[:, 0, g * LQ:(g + 1) * LQ], bank[:, g * LQ:(g + 1) * LQ],
                                          ACT.Identity, bias=bias[:, g:g + 1])
                last.then_inc(high_done, 1)

            def high_q(b):
                high(b, bank_b, bq_sb, q_parts, q_done, q_high)

            def high_k(b):
                high(b, bank_b, bk_sb, k_parts, k_done, k_high)

            def copy_v(b, par):
                act.wait_ge(v_done, PRIME + b + 1)
                act.activation(v_sb[:, par, :, :, 0:DK],
                               bank_a.rearrange("p (t h d) -> p t h d", t=KT, h=H), ACT.Copy).then_inc(v_ready, 1)

            inv_std1(0)
            copy_cT(0)
            act.wait_ge(qk_in, 16 * N_QK)
            high_k(0)
            copy_xT(0)
            inv_std1(1)
            high_q(0)
            copy_v(0, 0)
            copy_cT(1)
            act.wait_ge(k_laid[0], LAID)
            high_k(1)
            copy_xT(1)
            act.wait_ge(q_laid[0], LAID)
            high_q(1)
            copy_v(1, 1)
            inv_std1(2)

            def copy_u(b, par, n):
                act.wait_ge(pv_done, PRIME + HG * b + 2 * n + 2)
                act.wait_ge(uT_done, PRIME + QT * b - QT)
                act.activation(u_sb[:, par, 2 * n:2 * n + 2, :].rearrange("p g q -> p (g q)"), u_ps[n],
                               ACT.Copy).then_inc(u_copied, 1)

            def copy_aT(b):
                act.wait_ge(aT_done, PRIME + b + 1)
                act.wait_ge(wo_done, PRIME + b)
                act.activation(aT[:].rearrange("p k q -> p (k q)"), bank_a, ACT.Copy).then_inc(aT_ready, 1)

            def copy_x2T(b):
                act.wait_ge(x2T_done, PRIME + b + 1)
                act.activation(x2T[:, :, bass.ds(b * LQ, LQ)], u_ps[0].rearrange("p (k q) -> p k q", k=DT),
                               ACT.Copy).then_inc(x2T_ready, 1)

            def step(i, par, normed, project, first=False, last=False):
                b = 2 * i + par
                ip, pp = shift(i, par, 1)

                if project:
                    copy_cT(b + 2)
                for h in range(H):
                    act.wait_ge(sT_done, PRIME + H * b + h + 1)
                    if h % 4 == 0:
                        act.wait_ge(pv_done, PRIME + HG * b + h // 4 - 1)
                    act.activation(probs[:, h % ERING, :], sT_ps[h % 2].rearrange("p t q -> p (t q)"), ACT.Exp,
                                   scale=SCALE).then_inc(exp_done, 1)
                    if project and h == 3:
                        act.wait_ge(k_laid[pp], LAID * (ip + 1))
                        high_k(b + 2)
                    if project and h == 5:
                        copy_xT(b + 2)
                    if project and h == 9:
                        act.wait_ge(q_laid[pp], LAID * (ip + 1))
                        high_q(b + 2)
                    if h == 12:
                        copy_u(b, par, 0)
                    if not first and h == 13:
                        copy_aT(b - 1)
                    if normed and h == 14:
                        inv_std1(b + 3)
                copy_u(b, par, 1)
                if not first:
                    inv_std2(b - 1)
                if project:
                    copy_v(b + 2, par)
                if not first and not last:
                    copy_x2T(b - 1)

            step(0, 0, True, True, first=True)
            with act.Fori(0, B // 2 - 2) as i:
                step(i, 1, True, True)
                step(i + 1, 0, True, True)
            step(B // 2 - 2, 1, False, True)
            step(B // 2 - 1, 0, False, False)
            step(B // 2 - 1, 1, False, False, last=True)
            copy_aT(B - 1)
            copy_x2T(B - 2)

            def high_w13(e, i, par, c):
                act.wait_ge(w13_in[par], 64 * (i + 1))
                k, cols = piece(c)
                act.activation(w13_cut[par][:, 0, k, cols], w13[:, par, k, cols], ACT.Copy).then_inc(w13_high, 1)

            def high_x2(e, par, b0=0, b1=B):
                act.wait_ge(x2T_ready, PRIME + b1)
                act.activation(x2_cut[:, par, 0].rearrange("p k (b q) -> p k b q", b=B)[:, :, b0:b1],
                               tokens(e)[:, :, b0:b1], ACT.Copy).then_inc(x2_high, 1)

            for c in range(CUTS):
                high_w13(0, 0, 0, c)
            inv_std2(B - 1)
            high_x2(0, 0, 0, B - 1)
            copy_x2T(B - 1)
            high_x2(0, 0, B - 1, B)
            for c in range(CUTS):
                high_w13(1, 0, 1, c)

            def high_hid(e, par, m):
                act.wait_ge(hid_done, PRIME + FT * e + m + 1)
                act.activation(hid_cut[:, par, 0, m, :], hid[:, hid_slot(m), :], ACT.Copy).then_inc(hid_high, 1)

            def high_w2(e, i, par):
                act.wait_ge(w2_in[par], 32 * (i + 1))
                act.wait_ge(down_done, PRIME + e - 1)
                act.activation(w2_cut[:, par, 0], w2_sb[:, par], ACT.Copy).then_inc(w2_high, 1)

            def expert(e, i, par, more=True, first=False):
                ip, pp = shift(i, par, 1)
                for m in range(FT):
                    act.wait_ge(gu_done, FT * e + m + 1)
                    act.wait_ge(hid_done, PRIME + FT * e + m - 1)
                    rows = P if m < FM else FR
                    act.activation(silu[0:rows, m % 2, :], psum[0:rows, m, 0:B * TOK], ACT.Silu)\
                       .then_inc(silu_done, 1)
                    if m == 1:
                        act.wait_ge(down_done, PRIME + e - 1)
                    if m >= 1:
                        high_hid(e, par, m - 1)
                    if more and not first and m < CUTS:
                        high_w13(e + 1, ip, pp, m)
                    if more and m == CUTS:
                        high_x2(e + 1, pp)
                    if m == CUTS:
                        high_w2(e, i, par)
                high_hid(e, par, FT - 1)

            expert(0, 0, 0, first=True)
            with act.Fori(0, E // 2 - 1) as i:
                expert(2 * i + 1, i, 1)
                expert(2 * i + 2, i + 1, 0)
            expert(E - 1, E // 2 - 1, 1, more=False)

        @block.vector
        def _(dve):
            def stats(b, src, bn, mv, bn_done, stats_done):
                for t in range(QT):
                    last = dve.bn_stats(bn[:, t, :], src[:, t, :])
                last.then_inc(bn_done, 1)
                dve.wait_ge(bn_done, b + 1)
                settle(dve)
                for t in range(QT):
                    last = dve.bn_aggr(mv[:, t, :], bn[:, t, :])
                last.then_inc(stats_done, 1)

            def stats1(b):
                dve.wait_ge(x_loaded, 16 * (b + 1))
                dve.wait_ge(xn_ready, PRIME + b)
                stats(b, x_in, bn1, mv1, bn1_done, stats1_done)

            def rest(b, bank, bias, parts, left, high_done, parts_done, rest_done):
                dve.wait_ge(high_done, b + 1)
                dve.wait_ge(parts_done, PRIME + b)
                for g in range(2):
                    cols = slice(g * LQ, (g + 1) * LQ)
                    last = dve.scalar_tensor_tensor(out=left[:, cols], in0=bank[:, cols], scalar=bias[:, g:g + 1],
                                                    in1=parts[:, 0, cols], op0=ALU.add, op1=ALU.subtract)
                last.then_inc(rest_done, 1)

            def rest_q(b):
                rest(b, bank_b, bq_sb, q_parts, q_rest, q_high, q_parts_done, q_rest_done)

            def rest_k(b):
                rest(b, bank_b, bk_sb, k_parts, k_rest, k_high, k_parts_done, k_rest_done)

            def row_max(b, u):
                half, pair, t = u // 8, u % 8 // 2, u % 2
                dve.wait_ge(max_scores, 16 * b + u + 1)
                if u % 8 == 0:
                    dve.wait_ge(mT_done, PRIME + 2 * b + half - 1)
                dve.tensor_reduce(negmax[:, half, t, 2 * pair:2 * pair + 2], max_ps[u % 2], AX_X, ALU.max,
                                  negate=True).then_inc(max_done, 1)

            def max_parts(b, half):
                bank = (bank_b, bank_a)[half]
                dve.wait_ge(mT_done, PRIME + 2 * b + half + 1)
                dve.wait_ge(m_laid[half], PRIME + 16 * MROWS * b)
                dve.tensor_copy(mrow[:, half, 0, :], bank[0:H // 2, 0:LQ]).then_inc(m_high, 1)
                dve.wait_ge(m_high, 2 * b + half + 1)
                dve.tensor_tensor(mrow[:, half, 1, :], bank[0:H // 2, 0:LQ], mrow[:, half, 0, :], ALU.subtract)\
                   .then_inc(m_parts, 1)

            dve.memset(v_sb[:].rearrange("p a t h c -> p (a t h c)"), 0.0).then_inc(pads_zero, 1)
            stats1(0)
            dve.wait_ge(qk_in, 16 * N_QK)
            for g in range(2):
                last = dve.tensor_copy(wk_sb[:, g, :].rearrange("p (d h) -> p d h", d=DK),
                                       wk_nat[:].rearrange("p (h g d) -> p g d h", g=2, d=DK)[:, g])
            last.then_inc(perm_done, 1)
            for g in range(2):
                for k in range(DT):
                    last = dve.tensor_copy(wq_sb[:, k, g, :].rearrange("p (d h) -> p d h", d=DK),
                                           wq_nat[:, k, :].rearrange("p (h g d) -> p g d h", g=2, d=DK)[:, g])
            last.then_inc(perm_done, 1)
            rest_k(0)
            stats1(1)
            rest_q(0)
            dve.memset(hid[:, hid_slot(FM), :], 0.0).then_inc(pads_zero, 1)
            dve.memset(w2_sb[FR:P, :, FM, :], 0.0).then_inc(pads_zero, 1)
            dve.wait_ge(pads_zero, 3)
            dve.memset(v_sb[:, :, :, :, DK:DK + 1].rearrange("p a t h c -> p (a t h) c"), 1.0).then_inc(pads_zero, 1)
            dve.wait_ge(weights_in, 16 * N_WEIGHTS)
            dve.wait_ge(consts_ready, N_CONSTS)
            for k in range(DT):
                last = dve.tensor_scalar(bv_wide[:, k, :], ones[:], bv_col[:, k:k + 1], None, ALU.mult)
            last.then_inc(bvw_done, 1)
            rest_k(1)
            for u in range(UNITS - LATE):
                row_max(0, u)
                if u == 2:
                    rest_q(1)
                if u == 5:
                    stats1(2)
                if u == 8:
                    max_parts(0, 0)
            dve.wait_ge(bvo_done, 1)
            dve.tensor_tensor(bias_out[:], u_ps[0][:, 0:D], bo_row[:], ALU.add).then_inc(bvw_done, 1)
            dve.wait_ge(bvw_done, 2)
            dve.wait_ge(tanh_done, 1)
            dve.tensor_scalar(bias_out[:], bias_out[:], tanh_g[:, 0:1], None, ALU.mult).then_inc(bias_done, 1)

            def divide(b, t):
                bank = bank_a.rearrange("p (h c) -> p h c", h=H)
                dve.wait_ge(uT_done, PRIME + QT * b + t + 1)
                dve.reciprocal(rden[:, t, :], bank[:, :, DK]).then_inc(rden_done, 1)
                dve.wait_ge(rden_done, QT * b + t + 1)
                if t == 0:
                    dve.wait_ge(aT_done, PRIME + b)
                dve.tensor_tensor(attn[:, t, :].rearrange("p (h d) -> p h d", h=H), bank[:, :, 0:DK],
                                  rden[:, t, :].unsqueeze(2).to_broadcast([P, H, DK]), ALU.mult)\
                   .then_inc(attn_ready, 1)

            def residual(b):
                dve.wait_ge(wo_done, PRIME + b + 1)
                dve.wait_ge(res_ready, b + 1)
                dve.wait_ge(x1_stored, PRIME + 16 * b)
                dve.wait_ge(x2n_ready, PRIME + b)
                dve.scalar_tensor_tensor(out=x1[:].rearrange("p t d -> p (t d)"), in0=bank_a,
                                         scalar=tanh_g[:, 0:1], in1=x_res[:].rearrange("p t d -> p (t d)"),
                                         op0=ALU.mult, op1=ALU.add).then_inc(x1_ready, 1)
                dve.wait_ge(x1_ready, b + 1)
                stats(b, x1, bn2, mv2, bn2_done, stats2_done)

            def step(b, normed, project, maxima, first=False):
                row_max(b, 14)
                row_max(b, 15)
                max_parts(b, 1)
                for u in range(UNITS - LATE):
                    if maxima:
                        row_max(b + 1, u)
                    if project and u == 1:
                        rest_k(b + 2)
                    if normed and u == 4:
                        stats1(b + 3)
                    if not first and u == 5:
                        divide(b - 1, 0)
                    if project and u == 7:
                        rest_q(b + 2)
                    if not first and u == 7:
                        divide(b - 1, 1)
                    if maxima and u == 9:
                        max_parts(b + 1, 0)
                    if not first and u == 11:
                        residual(b - 1)

            step(0, True, True, True, first=True)
            with dve.Fori(0, B // 2 - 2) as i:
                step(2 * i + 1, True, True, True)
                step(2 * i + 2, True, True, True)
            step(B - 3, False, True, True)
            step(B - 2, False, False, True)
            step(B - 1, False, False, False)
            divide(B - 1, 0)
            divide(B - 1, 1)
            residual(B - 1)

            def low_w13(e, par, c):
                dve.wait_ge(w13_high, CUTS * e + c + 1)
                k, cols = piece(c)
                dve.tensor_tensor(w13_cut[par][:, 1, k, cols], w13[:, par, k, cols],
                                  w13_cut[par][:, 0, k, cols].bitcast(F32), ALU.subtract).then_inc(w13_low, 1)

            def low_w2(e, par):
                dve.wait_ge(w2_high, e + 1)
                dve.tensor_tensor(w2_cut[:, par, 1], w2_sb[:, par], w2_cut[:, par, 0].bitcast(F32), ALU.subtract)\
                   .then_inc(w2_low, 1)

            def hidden(e, par, more=True, first=False):
                for m in range(FT):
                    dve.wait_ge(silu_done, FT * e + m + 1)
                    dve.wait_ge(hid_low, PRIME + FT * e + m - 1)
                    if m < FM:
                        dve.tensor_tensor(hid[:, hid_slot(m), :], silu[:, m % 2, :], psum[:, m, B * TOK:2 * B * TOK],
                                          ALU.mult).then_inc(hid_done, 1)
                    else:
                        dve.tensor_tensor(hid[0:FR, hid_slot(m), :], silu[0:FR, m % 2, :], psum[FR:P, m, 0:B * TOK],
                                          ALU.mult).then_inc(hid_done, 1)
                    if more and not first and m < CUTS:
                        low_w13(e + 1, 1 - par, m)

            def finish(e, i, par):
                dve.wait_ge(down_done, PRIME + e + 1)
                dve.wait_ge(x1e_in[par], 32 * (i + 1))
                dve.wait_ge(out_stored[par], PRIME + 32 * i)
                dve.scalar_tensor_tensor(out=fin[:, par].rearrange("p n d -> p (n d)"), in0=down_ps[par],
                                         scalar=tanh_g[:, 1:2], in1=x1_e[:, par].rearrange("p n d -> p (n d)"),
                                         op0=ALU.mult, op1=ALU.add).then_inc(fin_done, 1)

            for e in range(2):
                for c in range(CUTS):
                    low_w13(e, e, c)
            hidden(0, 0, first=True)
            low_w2(0, 0)
            with dve.Fori(0, E // 2 - 1) as i:
                hidden(2 * i + 1, 1)
                low_w2(2 * i + 1, 1)
                finish(2 * i, i, 0)
                hidden(2 * i + 2, 0)
                low_w2(2 * i + 2, 0)
                finish(2 * i + 1, i, 1)
            hidden(E - 1, 1, more=False)
            low_w2(E - 1, 1)
            finish(E - 2, E // 2 - 1, 0)
            finish(E - 1, E // 2 - 1, 1)

        @block.tensor
        def _(pe):
            pe.wait_ge(consts_ready, N_CONSTS)

            def transpose_ctx(b):
                pe.wait_ge(ctx_loaded, 16 * (b + 1))
                for t in range(KT):
                    last = pe.transpose(bank_b[:, t * P:(t + 1) * P], ctx_in[:, t, :], ident[:])
                last.then_inc(cT_done, 1)

            def project_k(b):
                pe.wait_ge(cT_ready, b + 1)
                for g in range(2):
                    last = pe.matmul(bank_b[:, g * LKV:(g + 1) * LKV], wk_sb[:, g, :], cT[:], start=True, stop=True)
                last.then_inc(k_done, 1)

            def transpose_x(b):
                pe.wait_ge(xn_ready, PRIME + b + 1)
                for k in range(DT):
                    for t in range(QT):
                        last = pe.transpose(bank_a[:, k * LQ + t * P:k * LQ + (t + 1) * P],
                                            xn[:, t, k * P:(k + 1) * P], ident[:])
                last.then_inc(xT_done, 1)

            def project_q(b, g):
                pe.wait_ge(xT_ready, b + 1)
                pe.wait_ge(k_rest_done, b + 1)
                for k in range(DT):
                    last = pe.matmul(bank_b[:, g * LQ:(g + 1) * LQ], wq_sb[:, k, g, :], xT[:, k, :],
                                     start=(k == 0), stop=(k == DT - 1))
                if g == 1:
                    last.then_inc(q_done, 1)

            def project_v(b):
                pe.wait_ge(xT_ready, b + 1)
                for t in range(KT):
                    last = pe.matmul(bank_a[:, t * D:(t + 1) * D], cT[:, t * P:(t + 1) * P], wv_sb[:],
                                     start=True, stop=True)
                last.then_inc(v_done, 1)

            def score_max(i, par, u):
                b = 2 * i + par
                half, pair, t = u // 8, u % 8 // 2, u % 2
                if u == 0:
                    pe.wait_ge(q_laid[par], LAID * (i + 1))
                    pe.wait_ge(k_laid[par], LAID * (i + 1))
                pe.wait_ge(max_done, PRIME + 16 * b + u - 1)
                for n in range(2):
                    h = half * (H // 2) + 2 * pair + n
                    last = pe.matmul(max_ps[u % 2][:, n, :], q_st[0:ROWS, par, h * LQ + t * P:h * LQ + (t + 1) * P],
                                     k_st[0:ROWS, par, h * LKV:(h + 1) * LKV], start=True, stop=True)
                last.then_inc(max_scores, 1)

            def transpose_max(b, half):
                pe.wait_ge(max_done, PRIME + 16 * b + 8 * (half + 1))
                for t in range(QT):
                    last = pe.transpose((bank_b, bank_a)[half][0:H // 2, t * P:(t + 1) * P],
                                        negmax[:, half, t, :], ident[:])
                last.then_inc(mT_done, 1)

            for b in range(2):
                if b == 1:
                    pe.wait_ge(q_rest_done, 1)
                transpose_ctx(b)
                if b == 0:
                    pe.wait_ge(perm_done, 1)
                project_k(b)
                if b == 1:
                    pe.wait_ge(v_ready, 1)
                transpose_x(b)
                if b == 0:
                    pe.wait_ge(perm_done, 2)
                project_q(b, 0)
                project_q(b, 1)
                if b == 0:
                    pe.wait_ge(weights_in, 16 * N_WEIGHTS)
                project_v(b)
            pe.wait_ge(bvw_done, 1)
            for k in range(DT):
                last = pe.matmul(u_ps[0][:, 0:D], bv_wide[:, k, :], wo_sb[:, k, :], start=(k == 0), stop=(k == DT - 1))
            last.then_inc(bvo_done, 1)
            for u in range(UNITS - LATE):
                score_max(0, 0, u)
                if u == 7:
                    pe.wait_ge(q_rest_done, 2)
                    transpose_max(0, 0)
            pe.wait_ge(pads_done, 1)
            pe.wait_ge(pads_zero, 4)
            pe.wait_ge(bias_done, 1)

            def transpose_u(b, par, t):
                pe.wait_ge(u_copied, PRIME + 2 * b + 2)
                for g in range(HG):
                    last = pe.transpose(bank_a[:, g * P:(g + 1) * P],
                                        u_sb[:, par, g, t * P:(t + 1) * P], ident[:])
                last.then_inc(uT_done, 1)

            def transpose_attn(b):
                pe.wait_ge(attn_ready, QT * b + QT)
                for k in range(DT):
                    for t in range(QT):
                        last = pe.transpose(bank_a[:, k * LQ + t * P:k * LQ + (t + 1) * P],
                                            attn[:, t, k * P:(k + 1) * P], ident[:])
                last.then_inc(aT_done, 1)

            def project_out(b, t):
                pe.wait_ge(aT_ready, b + 1)
                for k in range(DT):
                    last = pe.matmul(bank_a[:, t * D:(t + 1) * D], aT[:, k, t * P:(t + 1) * P],
                                     wo_sb[:, k, :], start=(k == 0), stop=(k == DT - 1))
                if t == QT - 1:
                    last.then_inc(wo_done, 1)

            def transpose_x2(b):
                pe.wait_ge(x2n_ready, PRIME + b + 1)
                for k in range(DT):
                    for t in range(QT):
                        last = pe.transpose(u_ps[0][:, k * LQ + t * P:k * LQ + (t + 1) * P],
                                            x2n[:, t, k * P:(k + 1) * P], ident[:])
                last.then_inc(x2T_done, 1)

            def step(i, par, project, maxima, first=False, last=False):
                b = 2 * i + par

                def score(h):
                    if h % 8 == 0:
                        pe.wait_ge(m_laid[h // 8], PRIME + 16 * MROWS * (b + 1))
                    pe.wait_ge(exp_done, PRIME + H * b + h - 1)
                    for t in range(KT):
                        last = pe.matmul(sT_ps[h % 2][:, t, :],
                                         k_st[0:ROWS + MROWS, par, h * LKV + t * P:h * LKV + (t + 1) * P],
                                         q_st[0:ROWS + MROWS, par, h * LQ:(h + 1) * LQ], start=True, stop=True)
                    last.then_inc(sT_done, 1)

                def values(g, t):
                    if g == 0:
                        pe.wait_ge(v_ready, b + 1)
                    pe.wait_ge(exp_done, PRIME + H * b + 4 * g + 4)
                    if g == 0 and t == 0:
                        pe.wait_ge(u_copied, PRIME + 2 * b - 1)
                        pe.wait_ge(x2T_ready, PRIME + b - 1)
                    if g == 2 and t == 0:
                        pe.wait_ge(u_copied, PRIME + 2 * b)
                    for n in range(4):
                        h = 4 * g + n
                        last = pe.matmul(u_ps[g // 2][SLOT * n:SLOT * (n + 1), g % 2 * LQ:(g % 2 + 1) * LQ],
                                         v_sb[:, par, t, h, :], probs[:, h % ERING, t * LQ:(t + 1) * LQ],
                                         start=(t == 0), stop=(t == KT - 1))
                    if t == KT - 1:
                        last.then_inc(pv_done, 1)

                def maxi(u):
                    if maxima:
                        score_max(*shift(i, par, 1), u)

                if project:
                    pe.wait_ge(m_parts, 2 * b + 1)
                    transpose_ctx(b + 2)
                score(0)
                score(1)
                score_max(i, par, 14)
                score_max(i, par, 15)
                score(2)
                if not last:
                    pe.wait_ge(v_ready, b + 2)
                else:
                    pe.wait_ge(x1_ready, b - 1)
                transpose_max(b, 1)
                if project:
                    project_k(b + 2)
                score(3)
                maxi(0)
                if project:
                    pe.wait_ge(m_parts, 2 * b + 2)
                    transpose_x(b + 2)
                maxi(1)
                score(4)
                maxi(2)
                score(5)
                values(0, 0)
                maxi(3)
                score(6)
                values(0, 1)
                if project:
                    project_q(b + 2, 0)
                score(7)
                maxi(4)
                if project:
                    project_q(b + 2, 1)
                score(8)
                maxi(5)
                values(1, 0)
                if not first:
                    if project:
                        pe.wait_ge(xT_ready, b + 3)
                    else:
                        pe.wait_ge(m_parts, 2 * b + 2)
                    transpose_u(b - 1, 1 - par, 0)
                score(9)
                maxi(6)
                score(10)
                values(1, 1)
                maxi(7)
                score(11)
                if not first:
                    pe.wait_ge(attn_ready, QT * b - 1)
                    transpose_u(b - 1, 1 - par, 1)
                maxi(8)
                maxi(9)
                score(12)
                values(2, 0)
                score(13)
                if not first:
                    transpose_attn(b - 1)
                score(14)
                if maxima:
                    if project:
                        pe.wait_ge(q_rest_done, b + 3)
                    else:
                        pe.wait_ge(m_parts, 2 * b + 1)
                    transpose_max(b + 1, 0)
                score(15)
                if not first:
                    project_out(b - 1, 0)
                values(2, 1)
                maxi(10)
                maxi(11)
                if not first:
                    project_out(b - 1, 1)
                values(3, 0)
                values(3, 1)
                maxi(12)
                maxi(13)
                if project:
                    if not first:
                        pe.wait_ge(x1_ready, b)
                    project_v(b + 2)
                if not first and not last:
                    pe.wait_ge(u_copied, PRIME + 2 * b + 1)
                    transpose_x2(b - 1)

            step(0, 0, True, True, first=True)
            with pe.Fori(0, B // 2 - 2) as i:
                step(i, 1, True, True)
                step(i + 1, 0, True, True)
            step(B // 2 - 2, 1, True, True)
            step(B // 2 - 1, 0, False, True)
            step(B // 2 - 1, 1, False, False, last=True)
            pe.wait_ge(x1_ready, B - 1)
            transpose_u(B - 1, 1, 0)
            pe.wait_ge(attn_ready, QT * B - 1)
            transpose_u(B - 1, 1, 1)
            transpose_attn(B - 1)
            pe.wait_ge(u_copied, PRIME + 2 * B - 1)
            transpose_x2(B - 2)
            project_out(B - 1, 0)
            project_out(B - 1, 1)
            pe.wait_ge(x2T_ready, PRIME + B - 1)
            transpose_x2(B - 1)

            pe.wait_ge(x2T_ready, PRIME + B)

            def gate_up(e, par):
                pe.wait_ge(w13_low, CUTS * (e + 1))
                pe.wait_ge(x2_low, e + 2)
                for m in range(FT):
                    pe.wait_ge(hid_done, PRIME + FT * e + m + 1 - FT)
                    for n in range(2 if m < FM else 1):
                        c = n * FM * P + m * P if m < FM else 2 * FM * P
                        for k in range(DT):
                            for wp, xp in SPLIT:
                                last = pe.matmul(psum[:, m, n * B * TOK:(n + 1) * B * TOK],
                                                 w13_cut[par][:, wp, k, c:c + P], x2_cut[:, par, xp, k, :],
                                                 start=(k == 0 and (wp, xp) == SPLIT[0]),
                                                 stop=(k == DT - 1 and (wp, xp) == SPLIT[-1]))
                    last.then_inc(gu_done, 1)

            def down(e, par):
                pe.wait_ge(w2_low, e + 1)
                pe.wait_ge(fin_done, PRIME + e - 1)
                for n in range(2):
                    for m in range(FT):
                        pe.wait_ge(hid_low, PRIME + FT * e + m + 1)
                        for hp, wp in SPLIT:
                            last = pe.matmul(down_ps[par][:, n * D:(n + 1) * D],
                                             hid_cut[:, par, hp, m, n * P:(n + 1) * P], w2_cut[:, par, wp, m, :],
                                             start=(m == 0 and (hp, wp) == SPLIT[0]),
                                             stop=(m == FT - 1 and (hp, wp) == SPLIT[-1]))
                last.then_inc(down_done, 1)

            gate_up(0, 0)
            gate_up(1, 1)
            down(0, 0)
            with pe.Fori(1, E // 2) as i:
                gate_up(2 * i, 0)
                down(2 * i - 1, 1)
                gate_up(2 * i + 1, 1)
                down(2 * i, 0)
            down(E - 1, 1)


_INS = ["x", "ctx_512", "g_xattn", "g_ffn", "L0_xattn_Wq", "L0_xattn_bq", "L0_xattn_Wk", "L0_xattn_bk",
        "L0_xattn_Wv", "L0_xattn_bv", "L0_xattn_Wo", "L0_xattn_bo", "L0_ffn_w1", "L0_ffn_w3", "L0_ffn_w2"]
_OUTS = [((8, 256, 256), "float32")]


def kernel(**inputs):
    import numpy as _np
    import concourse.bacc as _bacc
    from concourse import mybir as _mybir
    from concourse.bass_utils import run_bass_kernel_spmd as _run

    nc = _bacc.Bacc("TRN2", target_bir_lowering=False, num_devices=1)
    arrays, args = {}, []
    for name in _INS:
        a = _np.ascontiguousarray(inputs[name])
        arrays[f"in_{name}"] = a
        args.append(nc.dram_tensor(f"in_{name}", a.shape, _mybir.dt.from_np(a.dtype), kind="ExternalInput").ap())
    for i, (shape, dtype) in enumerate(_OUTS):
        dt = _mybir.dt.from_np(_np.dtype(dtype))
        args.append(nc.dram_tensor(f"out_{i}", shape, dt, kind="ExternalOutput").ap())
    gated_xattn_expert_ffn(nc, *args)
    r = _run(nc, [arrays], core_ids=[0])
    return r.results[0]["out_0"]
```
